# Optimizing a Trainium2 kernel written in Bass

```python
import numpy as np
import jax
import jax.numpy as jnp

def _softmax(x, axis=-1):
    return jax.nn.softmax(x, axis=axis)

def _gelu(x):
    return jax.nn.gelu(x, approximate=True)

def _silu(x):
    return jax.nn.silu(x)

def _sigmoid(x):
    return jax.nn.sigmoid(x)

def _layernorm(x, axis=-1, eps=1e-05):
    m = jnp.mean(x, axis=axis, keepdims=True)
    v = jnp.var(x, axis=axis, keepdims=True)
    return (x - m) / jnp.sqrt(v + eps)

def _scatter_add(tgt, idx, src, axis=0):
    return tgt.at[idx].add(src)

def _segment_sum(src, seg, n):
    return jax.ops.segment_sum(src, seg, n)
kernel_name = 'mk_xattn_ffn_d2_seqx_r4_4a0068'

def setup_inputs(seed: int=0):
    np.random.seed(seed)
    _w = jnp.asarray

    def _rec_inputs():
        import jax
        import jax.numpy as jnp
        _rk = jax.random.key(seed)
        x = 0.0003765 + 1 * jax.random.normal(jax.random.fold_in(_rk, 1), (16, 256, 256), jnp.float32)
        _lenS = 256 - jax.random.randint(jax.random.fold_in(_rk, 7), (16,), 0, max(1, 256 // 4) + 1, jnp.int32)
        _lenS2 = 256 - jax.random.randint(jax.random.fold_in(_rk, 8), (16,), 0, max(1, 256 // 4) + 1, jnp.int32)
        _ctx_1024P = jax.random.normal(jax.random.fold_in(_rk, 11), (16, 16, 256), jnp.float32)
        _ctx_1024c = jax.random.dirichlet(jax.random.fold_in(_rk, 511), 0.3 * jnp.ones((16,), jnp.float32), (16, 256))
        _ctx_1024t = jnp.einsum('bsk,bkd->bsd', _ctx_1024c, _ctx_1024P)
        _ctx_1024t = _ctx_1024t * jax.lax.rsqrt(jnp.mean(jnp.square(_ctx_1024t)) + 1e-12) * 0.953939
        ctx_1024 = -0.000292821 + 1.00034 * (_ctx_1024t + 0.3 * jax.random.normal(jax.random.fold_in(_rk, 611), (16, 256, 256), jnp.float32))
        _validS = jnp.arange(256)[None, :] < _lenS[:, None]
        _validS2 = jnp.arange(256)[None, :] < _lenS2[:, None]
        _causal = jnp.tril(jnp.ones((256, 256), dtype=bool))
        mask_Bx1xSxS2_ik1 = jnp.where(jnp.broadcast_to(_validS2[:, None, None, :], (16, 1, 256, 256)), 1, 0).astype(jnp.int32)
        return (x, ctx_1024, mask_Bx1xSxS2_ik1)
    x, ctx_1024, mask_Bx1xSxS2_ik1 = _rec_inputs()

    def _L0_xattn_setup():
        import jax, jax.numpy as jnp
        import numpy as np
        B, L, E, H = (2, 512, 256, 16)
        D = E // H
        key = jax.random.key(seed)
        ks = jax.random.split(key, 6)
        values = jax.random.normal(ks[0], (B, L, E), dtype=jnp.float32)
        keys = jax.random.normal(ks[1], (B, L, E), dtype=jnp.float32)
        query = jax.random.normal(ks[2], (B, L, E), dtype=jnp.float32)
        mask = jax.random.randint(ks[3], (B, 1, L, L), 0, 2, dtype=jnp.int32)
        W_out = jax.random.normal(ks[4], (E, E), dtype=jnp.float32) * 0.02
        b_out = jax.random.normal(ks[5], (E,), dtype=jnp.float32) * 0.02
        return {'values': values, 'keys': keys, 'query': query, 'mask': mask, 'W_out': W_out, 'b_out': b_out}
    _L0_xattn_all = _L0_xattn_setup()
    _L0_xattn_in = {k: v for k, v in _L0_xattn_all.items() if k in ('W_out', 'b_out')}
    del _L0_xattn_all

    def _L0_ffn_setup():
        import jax, jax.numpy as jnp
        import numpy as np
        EPS = 1e-08

        def _ste(x, q):
            return x + jax.lax.stop_gradient(q - x)

        def quant_act_uint8(x):
            s = jax.lax.stop_gradient(jnp.maximum(jnp.max(x), EPS)) / 255.0
            q = jnp.clip(jnp.round(x / s), 0.0, 255.0) * s
            return (_ste(x, q), s)

        def quant_weight_int8_perchannel(w):
            s = jax.lax.stop_gradient(jnp.maximum(jnp.max(jnp.abs(w), axis=1, keepdims=True), EPS)) / 127.0
            q = jnp.clip(jnp.round(w / s), -128.0, 127.0) * s
            return (_ste(w, q), s[:, 0])

        def quant_bias_int32(b, s_in, s_w):
            s = jax.lax.stop_gradient(s_in * s_w)
            q = jnp.round(b / s) * s
            return _ste(b, q)

        def quant_linear(x, w, b):
            xq, s_in = quant_act_uint8(x)
            wq, s_w = quant_weight_int8_perchannel(w)
            bq = quant_bias_int32(b, s_in, s_w)
            return jnp.einsum('btd,fd->btf', xq, wq) + bq
        key = jax.random.key(seed)
        k1, k2, k3, k4, k5 = jax.random.split(key, 5)
        B, S, D, F = (4, 512, 256, 1024)
        return {'x': jax.random.normal(k1, (B, S, D), dtype=jnp.float32), 'w1': jax.random.normal(k2, (F, D), dtype=jnp.float32) * (1.0 / np.sqrt(D)), 'b1': jax.random.normal(k3, (F,), dtype=jnp.float32) * 0.01, 'w2': jax.random.normal(k4, (D, F), dtype=jnp.float32) * (1.0 / np.sqrt(F)), 'b2': jax.random.normal(k5, (D,), dtype=jnp.float32) * 0.01}
    _L0_ffn_all = _L0_ffn_setup()
    _L0_ffn_in = {k: v for k, v in _L0_ffn_all.items() if k in ('w1', 'b1', 'w2', 'b2')}
    del _L0_ffn_all

    def _L1_xattn_setup():
        import jax, jax.numpy as jnp
        import numpy as np
        import math
        B, L, D, H = (8, 512, 256, 16)
        E = D // H
        FACTOR = 1
        TOP_K = int(FACTOR * math.log(L))
        key = jax.random.key(seed)
        ks = jax.random.split(key, 11)
        s = 1.0 / math.sqrt(D)
        f32 = jnp.float32
        return {'queries': jax.random.normal(ks[0], (B, L, D), f32), 'keys': jax.random.normal(ks[1], (B, L, D), f32), 'values': jax.random.normal(ks[2], (B, L, D), f32), 'Wq': jax.random.normal(ks[3], (D, D), f32) * s, 'bq': jax.random.normal(ks[4], (D,), f32) * 0.01, 'Wk': jax.random.normal(ks[5], (D, D), f32) * s, 'bk': jax.random.normal(ks[6], (D,), f32) * 0.01, 'Wv': jax.random.normal(ks[7], (D, D), f32) * s, 'bv': jax.random.normal(ks[8], (D,), f32) * 0.01, 'Wo': jax.random.normal(ks[9], (D, D), f32) * s, 'bo': jax.random.normal(ks[10], (D,), f32) * 0.01}
    _L1_xattn_all = _L1_xattn_setup()
    _L1_xattn_in = {k: v for k, v in _L1_xattn_all.items() if k in ('Wq', 'bq', 'Wk', 'bk', 'Wv', 'bv', 'Wo', 'bo')}
    del _L1_xattn_all

    def _L1_ffn_setup():
        import jax, jax.numpy as jnp
        import numpy as np
        import math
        N_EMBD = 256
        HIDDEN = 4 * N_EMBD
        N_EXPERTS = 8
        TOP_K = 2
        B, T = (4, 512)

        def new_gelu(x):
            c = math.sqrt(2.0 / math.pi)
            return 0.5 * x * (1.0 + jnp.tanh(c * (x + 0.044715 * x * x * x)))

        def _moe_forward(x, Wfc_s, bfc_s, Wproj_s, bproj_s, Wr, Wfc, bfc, Wproj, bproj):
            Bb, Tt, C = x.shape
            xf = x.reshape(Bb * Tt, C)
            N = Bb * Tt
            shared = new_gelu(xf @ Wfc_s + bfc_s) @ Wproj_s + bproj_s
            logits = xf @ Wr
            probs = jax.nn.softmax(logits, axis=-1)
            topk_p, topk_i = jax.lax.top_k(probs, TOP_K)
            topk_p = topk_p / jnp.sum(topk_p, axis=-1, keepdims=True)
            gate = jnp.zeros((N, N_EXPERTS), dtype=xf.dtype)
            gate = gate.at[jnp.arange(N)[:, None], topk_i].add(topk_p)
            routed = jnp.zeros_like(xf)
            for e in range(N_EXPERTS):
                h = new_gelu(xf @ Wfc[e] + bfc[e]) @ Wproj[e] + bproj[e]
                routed = routed + h * gate[:, e:e + 1]
            return (shared + routed).reshape(Bb, Tt, C)
        key = jax.random.key(seed)
        ks = jax.random.split(key, 10)
        s = 0.02
        return {'x': jax.random.normal(ks[0], (B, T, N_EMBD), dtype=jnp.float32), 'Wfc_s': jax.random.normal(ks[1], (N_EMBD, HIDDEN), dtype=jnp.float32) * s, 'bfc_s': jnp.zeros((HIDDEN,), dtype=jnp.float32), 'Wproj_s': jax.random.normal(ks[2], (HIDDEN, N_EMBD), dtype=jnp.float32) * s, 'bproj_s': jnp.zeros((N_EMBD,), dtype=jnp.float32), 'Wr': jax.random.normal(ks[3], (N_EMBD, N_EXPERTS), dtype=jnp.float32) * s, 'Wfc': jax.random.normal(ks[4], (N_EXPERTS, N_EMBD, HIDDEN), dtype=jnp.float32) * s, 'bfc': jnp.zeros((N_EXPERTS, HIDDEN), dtype=jnp.float32), 'Wproj': jax.random.normal(ks[5], (N_EXPERTS, HIDDEN, N_EMBD), dtype=jnp.float32) * s, 'bproj': jnp.zeros((N_EXPERTS, N_EMBD), dtype=jnp.float32)}
    _L1_ffn_all = _L1_ffn_setup()
    _L1_ffn_in = {k: v for k, v in _L1_ffn_all.items() if k in ('Wfc_s', 'bfc_s', 'Wproj_s', 'bproj_s', 'Wr', 'Wfc', 'bfc', 'Wproj', 'bproj')}
    del _L1_ffn_all
    return {'x': x, 'ctx_1024': ctx_1024, 'mask_Bx1xSxS2_ik1': mask_Bx1xSxS2_ik1, 'L0_xattn_W_out': _L0_xattn_in['W_out'], 'L0_xattn_b_out': _L0_xattn_in['b_out'], 'L0_ffn_w1': _L0_ffn_in['w1'], 'L0_ffn_b1': _L0_ffn_in['b1'], 'L0_ffn_w2': _L0_ffn_in['w2'], 'L0_ffn_b2': _L0_ffn_in['b2'], 'L1_xattn_Wq': _L1_xattn_in['Wq'], 'L1_xattn_bq': _L1_xattn_in['bq'], 'L1_xattn_Wk': _L1_xattn_in['Wk'], 'L1_xattn_bk': _L1_xattn_in['bk'], 'L1_xattn_Wv': _L1_xattn_in['Wv'], 'L1_xattn_bv': _L1_xattn_in['bv'], 'L1_xattn_Wo': _L1_xattn_in['Wo'], 'L1_xattn_bo': _L1_xattn_in['bo'], 'L1_ffn_Wfc_s': _L1_ffn_in['Wfc_s'], 'L1_ffn_bfc_s': _L1_ffn_in['bfc_s'], 'L1_ffn_Wproj_s': _L1_ffn_in['Wproj_s'], 'L1_ffn_bproj_s': _L1_ffn_in['bproj_s'], 'L1_ffn_Wr': _L1_ffn_in['Wr'], 'L1_ffn_Wfc': _L1_ffn_in['Wfc'], 'L1_ffn_bfc': _L1_ffn_in['bfc'], 'L1_ffn_Wproj': _L1_ffn_in['Wproj'], 'L1_ffn_bproj': _L1_ffn_in['bproj']}

def reference(x, ctx_1024, mask_Bx1xSxS2_ik1, L0_xattn_W_out, L0_xattn_b_out, L0_ffn_w1, L0_ffn_b1, L0_ffn_w2, L0_ffn_b2, L1_xattn_Wq, L1_xattn_bq, L1_xattn_Wk, L1_xattn_bk, L1_xattn_Wv, L1_xattn_bv, L1_xattn_Wo, L1_xattn_bo, L1_ffn_Wfc_s, L1_ffn_bfc_s, L1_ffn_Wproj_s, L1_ffn_bproj_s, L1_ffn_Wr, L1_ffn_Wfc, L1_ffn_bfc, L1_ffn_Wproj, L1_ffn_bproj):
    import jax
    import jax.numpy as jnp

    def _L0_xattn_ref(values, keys, query, mask, W_out, b_out):
        import jax, jax.numpy as jnp
        import numpy as np
        B, L, E, H = (2, 512, 256, 16)
        D = E // H
        b, l, e = query.shape
        v = values.reshape(b, l, H, D)
        k = keys.reshape(b, l, H, D)
        q = query.reshape(b, l, H, D)
        scores = jnp.einsum('bqhd,bkhd->bhqk', q, k)
        scores = jnp.where(mask == 0, jnp.float32(-1e+20), scores)
        attn = jax.nn.softmax(scores / jnp.float32(E ** 0.5), axis=3)
        out = jnp.einsum('bhqk,bkhd->bqhd', attn, v).reshape(b, l, e)
        out = out @ W_out.T + b_out
        return out

    def _L0_ffn_ref(x, w1, b1, w2, b2):
        import jax, jax.numpy as jnp
        import numpy as np
        EPS = 1e-08

        def _ste(x, q):
            return x + jax.lax.stop_gradient(q - x)

        def quant_act_uint8(x):
            s = jax.lax.stop_gradient(jnp.maximum(jnp.max(x), EPS)) / 255.0
            q = jnp.clip(jnp.round(x / s), 0.0, 255.0) * s
            return (_ste(x, q), s)

        def quant_weight_int8_perchannel(w):
            s = jax.lax.stop_gradient(jnp.maximum(jnp.max(jnp.abs(w), axis=1, keepdims=True), EPS)) / 127.0
            q = jnp.clip(jnp.round(w / s), -128.0, 127.0) * s
            return (_ste(w, q), s[:, 0])

        def quant_bias_int32(b, s_in, s_w):
            s = jax.lax.stop_gradient(s_in * s_w)
            q = jnp.round(b / s) * s
            return _ste(b, q)

        def quant_linear(x, w, b):
            xq, s_in = quant_act_uint8(x)
            wq, s_w = quant_weight_int8_perchannel(w)
            bq = quant_bias_int32(b, s_in, s_w)
            return jnp.einsum('btd,fd->btf', xq, wq) + bq
        h = jax.nn.relu(quant_linear(x, w1, b1))
        return quant_linear(h, w2, b2)

    def _L1_xattn_ref(queries, keys, values, Wq, bq, Wk, bk, Wv, bv, Wo, bo):
        import jax, jax.numpy as jnp
        import numpy as np
        import math
        B, L, D, H = (8, 512, 256, 16)
        E = D // H
        FACTOR = 1
        TOP_K = int(FACTOR * math.log(L))
        Bq, Lq, Dq = queries.shape
        q = (queries @ Wq + bq).reshape(Bq, Lq, H, E).transpose(0, 2, 3, 1)
        k = (keys @ Wk + bk).reshape(Bq, Lq, H, E).transpose(0, 2, 3, 1)
        v = (values @ Wv + bv).reshape(Bq, Lq, H, E).transpose(0, 2, 3, 1)
        q_fft = jnp.fft.rfft(q, axis=-1)
        k_fft = jnp.fft.rfft(k, axis=-1)
        corr = jnp.fft.irfft(q_fft * jnp.conj(k_fft), n=Lq, axis=-1)
        mean_value = corr.mean(axis=(1, 2))
        _, index = jax.lax.top_k(mean_value.mean(axis=0), TOP_K)
        weights = mean_value[:, index]
        tmp_corr = jax.nn.softmax(weights, axis=-1)
        idx = (jnp.arange(Lq)[None, :] + index[:, None]) % Lq
        gathered = v[..., idx]
        agg = jnp.einsum('bhekl,bk->bhel', gathered, tmp_corr)
        out = agg.transpose(0, 3, 1, 2).reshape(Bq, Lq, Dq)
        return out @ Wo + bo

    def _L1_ffn_ref(x, Wfc_s, bfc_s, Wproj_s, bproj_s, Wr, Wfc, bfc, Wproj, bproj):
        import jax, jax.numpy as jnp
        import numpy as np
        import math
        N_EMBD = 256
        HIDDEN = 4 * N_EMBD
        N_EXPERTS = 8
        TOP_K = 2
        B, T = (4, 512)

        def new_gelu(x):
            c = math.sqrt(2.0 / math.pi)
            return 0.5 * x * (1.0 + jnp.tanh(c * (x + 0.044715 * x * x * x)))

        def _moe_forward(x, Wfc_s, bfc_s, Wproj_s, bproj_s, Wr, Wfc, bfc, Wproj, bproj):
            Bb, Tt, C = x.shape
            xf = x.reshape(Bb * Tt, C)
            N = Bb * Tt
            shared = new_gelu(xf @ Wfc_s + bfc_s) @ Wproj_s + bproj_s
            logits = xf @ Wr
            probs = jax.nn.softmax(logits, axis=-1)
            topk_p, topk_i = jax.lax.top_k(probs, TOP_K)
            topk_p = topk_p / jnp.sum(topk_p, axis=-1, keepdims=True)
            gate = jnp.zeros((N, N_EXPERTS), dtype=xf.dtype)
            gate = gate.at[jnp.arange(N)[:, None], topk_i].add(topk_p)
            routed = jnp.zeros_like(xf)
            for e in range(N_EXPERTS):
                h = new_gelu(xf @ Wfc[e] + bfc[e]) @ Wproj[e] + bproj[e]
                routed = routed + h * gate[:, e:e + 1]
            return (shared + routed).reshape(Bb, Tt, C)
        return _moe_forward(x, Wfc_s, bfc_s, Wproj_s, bproj_s, Wr, Wfc, bfc, Wproj, bproj)
    x = x + _L0_xattn_ref(ctx_1024, ctx_1024, _layernorm(x, axis=-1), mask_Bx1xSxS2_ik1, L0_xattn_W_out, L0_xattn_b_out)
    x = x + _L0_ffn_ref(_layernorm(x, axis=-1), L0_ffn_w1, L0_ffn_b1, L0_ffn_w2, L0_ffn_b2)
    x = x + _L1_xattn_ref(_layernorm(x, axis=-1), ctx_1024, ctx_1024, L1_xattn_Wq, L1_xattn_bq, L1_xattn_Wk, L1_xattn_bk, L1_xattn_Wv, L1_xattn_bv, L1_xattn_Wo, L1_xattn_bo)
    x = x + _L1_ffn_ref(_layernorm(x, axis=-1), L1_ffn_Wfc_s, L1_ffn_bfc_s, L1_ffn_Wproj_s, L1_ffn_bproj_s, L1_ffn_Wr, L1_ffn_Wfc, L1_ffn_bfc, L1_ffn_Wproj, L1_ffn_bproj)
    return x

_drawn_inputs = setup_inputs


def setup_inputs(seed=0):
    import zlib

    import numpy as np

    out = dict(_drawn_inputs(seed))
    spreads = {'L1_ffn_bfc_s': (0.0, 0.29),
     'L1_ffn_bproj_s': (0.0, 0.1),
     'L1_ffn_bfc': (0.0, 0.434),
     'L1_ffn_bproj': (0.0, 0.1)}
    factors = {'L0_xattn_b_out': 2.767,
     'L0_ffn_b1': 5.198,
     'L0_ffn_b2': 6.292,
     'L1_xattn_bq': 8.0,
     'L1_xattn_bk': 8.0,
     'L1_xattn_bv': 6.23,
     'L1_xattn_bo': 5.757}
    for name, (base, spread) in spreads.items():
        noise = np.random.default_rng([zlib.crc32(name.encode()), seed]).standard_normal(out[name].shape)
        drawn = base * np.exp(spread * noise) if base else spread * noise
        out[name] = jnp.asarray(drawn.astype(out[name].dtype))
    for name, factor in factors.items():
        out[name] = (out[name] * factor).astype(out[name].dtype)
    return out
```

```python
from contextlib import ExitStack

import concourse.bass as bass
from concourse import mybir

F32 = mybir.dt.float32
F16 = mybir.dt.float16
BF16 = mybir.dt.bfloat16
I32 = mybir.dt.int32
ALU = mybir.AluOpType
ACT = mybir.ActivationFunctionType
AX = mybir.AxisListType

P = 128
STAGE_FROM = 0
STAGE_TO = 9


def wait(eng, sem, value):
    if isinstance(value, int) and value <= 0:
        return
    eng.wait_ge(sem, value)


def wait_apart(eng, passed, sem, value):
    if isinstance(value, int):
        return wait(eng, sem, value)
    eng.wait_ge(sem, value)
    eng.sem_inc(passed, 1)


class Shape:

    def __init__(self, d):
        self.NB, self.S, self.D = d["x"].shape
        self.NQ = self.S // P
        self.NT = self.NB * self.NQ


EPS = 1e-5
LN_STEPS = 12
WSCALE = 256.0


def ln_memory(ctx, nc, NT):
    m = {}
    for name, shape in (("stats", [P, NT, 6]), ("ln_a", [P, NT]), ("ln_b", [P, NT]), ("ln_std", [P, NT]),
                        ("rstd", [P, NT]), ("nmr", [P, NT])):
        m[name] = ctx.enter_context(nc.sbuf_tensor(name, shape, F32))
    m["s_lnv"] = ctx.enter_context(nc.semaphore("ln_vector_step"))
    m["s_lns"] = ctx.enter_context(nc.semaphore("ln_std_ready"))
    return m


def ln_scalar(act, m, NT, number):
    act.wait_ge(m["s_lnv"], number * (NT + LN_STEPS) + NT + 6)
    act.activation(m["ln_std"][:], m["ln_b"][:], ACT.Sqrt).then_inc(m["s_lns"], 1)


def ln_vector(v, m, X, NT, D, number):
    stats, ln_a, ln_b, rstd, nmr = (m[k] for k in ("stats", "ln_a", "ln_b", "rstd", "nmr"))
    with v.Fori(0, NT) as t:
        v.bn_stats(stats[:, t, :], X[:, t, :]).then_inc(m["s_lnv"], 1)
    done = number * (NT + LN_STEPS) + NT

    def link(ins):
        nonlocal done
        ins.then_inc(m["s_lnv"], 1)
        done += 1
        v.wait_ge(m["s_lnv"], done)

    v.wait_ge(m["s_lnv"], done)
    link(v.tensor_tensor(ln_a[:], stats[:, :, 1], stats[:, :, 4], ALU.subtract))
    link(v.tensor_tensor(nmr[:], stats[:, :, 1], stats[:, :, 4], ALU.add))
    link(v.tensor_tensor(ln_b[:], stats[:, :, 2], stats[:, :, 5], ALU.add))
    link(v.scalar_tensor_tensor(ln_a[:], ln_a[:], 0.25, ln_a[:], ALU.mult, ALU.mult))
    link(v.scalar_tensor_tensor(ln_b[:], ln_b[:], 1.0 / D, ln_a[:], ALU.mult, ALU.add))
    link(v.tensor_scalar(ln_b[:], ln_b[:], EPS, None, ALU.add))
    v.wait_ge(m["s_lns"], number + 1)
    link(v.reciprocal(rstd[:], m["ln_std"][:]))
    link(v.tensor_tensor(ln_a[:], rstd[:], rstd[:], ALU.mult))
    link(v.tensor_tensor(ln_a[:], ln_a[:], ln_b[:], ALU.mult))
    link(v.tensor_scalar(ln_a[:], ln_a[:], -0.5, 1.5, ALU.mult, ALU.add))
    link(v.tensor_tensor(rstd[:], rstd[:], ln_a[:], ALU.mult))
    link(v.scalar_tensor_tensor(nmr[:], nmr[:], -0.5, rstd[:], ALU.mult, ALU.mult))


def attention(nc, d, g, X, ident, banks, halves_dram):
    NB, S, D, NQ, NT = g.NB, g.S, g.D, g.NQ, g.NT
    H, DH = 16, 16
    HP = H // 2
    SPLIT = 4 * DH
    UNITS = NQ * HP
    SCALE = 1.0 / D ** 0.5

    with ExitStack() as ctx:
        def sb(name, shape, dt=F32):
            return ctx.enter_context(nc.sbuf_tensor(name, shape, dt))

        def sem(name):
            return ctx.enter_context(nc.semaphore(name))

        bank = [banks[i // 2][:, (i % 2) * 512:(i % 2) * 512 + 512] for i in range(8)]
        ln = g.ln
        rstd, nmr = ln["rstd"], ln["nmr"]
        ident16 = sb("ident16", [P, P], F16)

        woT = sb("woT", [P, 2, D])
        bo_bc = sb("bo_bc", [P, D])
        ctx_rows = [sb(f"ctx_rows{s}", [P, NQ, D]) for s in range(2)]
        mask_int = [sb(f"mask_int{s}", [P, NQ, S], I32) for s in range(2)]
        mask_bias = [sb(f"mask_bias{s}", [P, NQ, S]) for s in range(2)]
        q_rows = [sb(f"q_rows{s}", [P, NQ, D]) for s in range(2)]
        k_split = [sb(f"k_split{s}", [P, NQ, H, 4, DH], F16) for s in range(2)]
        q_split = [sb(f"q_split{s}", [P, NQ, H, 4, DH], F16) for s in range(2)]
        kT = [sb(f"kT{s}", [P, 2, HP, S], F16) for s in range(2)]
        qT = [sb(f"qT{s}", [P, HP, S], F16) for s in range(2)]
        scores = [sb(f"scores{s}", [P, 2, S]) for s in range(2)]
        row_max = [sb(f"row_max{s}", [P, 2]) for s in range(2)]
        neg_max = [sb(f"neg_max{s}", [P, 2]) for s in range(2)]
        probs = [sb(f"probs{s}", [P, 2, S]) for s in range(2)]
        row_sum = [sb(f"row_sum{s}", [P, H]) for s in range(NQ)]
        row_rec = sb("row_rec", [P, H])
        p_hi = [sb(f"p_hi{s}", [P, 2, NQ, P], F16) for s in range(4)]
        p_lo = [sb(f"p_lo{s}", [P, 2, NQ, P], F16) for s in range(4)]
        o_sum = sb("o_sum", [P, H, DH])
        o_rows = [sb(f"o_rows{s}", [P, D]) for s in range(2)]
        oT = sb("oT", [P, 2, P])
        NE, _, F = d["L1_ffn_Wfc"].shape
        HALF = D * F // P
        w_in = [sb(f"w_in{s}", [P, HALF]) for s in range(2)]
        w_cut = [sb(f"w_cut{s}", [P, 2, HALF], F16) for s in range(2)]

        s_const = sem("const_in")
        s_x = sem("x_in")
        s_ctx = [sem(f"ctx_in{s}") for s in range(2)]
        s_mask = [sem(f"mask_in{s}") for s in range(2)]
        s_id16 = sem("ident16_ready")
        s_kzero = sem("kT_zeroed")
        s_khi = sem("k_hi_written")
        s_klo = sem("k_lo_written")
        s_kdup = sem("k_split_ready")
        s_qhi = sem("q_hi_written")
        s_qlo = sem("q_lo_written")
        s_qdup = sem("q_split_ready")
        s_bias = sem("out_bias_added")
        s_mb = sem("mask_bias_ready")
        s_qn = sem("q_rows_ready")
        s_fillT = sem("split_transposed")
        s_fill = sem("split_copied")
        s_S = sem("scores_in_psum")
        s_ttr = sem("scores_masked")
        s_nm = sem("neg_max_ready")
        s_exp = sem("probs_ready")
        s_T = sem("probs_transposed")
        s_cast = sem("p_hi_ready")
        s_sub = sem("p_lo_ready")
        s_PV = sem("values_weighted")
        s_rec = sem("row_rec_ready")
        s_osum = sem("o_sum_ready")
        s_on = sem("o_rows_ready")
        s_oTp = sem("o_transposed")
        s_oT = sem("oT_ready")
        s_op = sem("projected")
        s_xadd = sem("x_added")

        s_passed_v, s_passed_p = g.passed_vector, g.passed_pool

        s_wi = [sem(f"moe_half_in{s}") for s in range(2)]
        s_wc = sem("moe_half_cut")
        s_ws = [sem(f"moe_half_stored{s}") for s in range(2)]

        psum_s = bank[0:2]
        psum_t = bank[2:4]
        psum_o = bank[4:6]
        psum_fill = bank[6]
        psum_w = bank[7]

        x_view = d["x"].rearrange("b (t p) c -> p (b t) c", p=P)
        ctx_view = d["ctx_1024"].rearrange("b (t p) c -> p b t c", p=P)
        mask_view = d["mask_Bx1xSxS2_ik1"].rearrange("b o (t p) k -> p (b o) t k", p=P)

        block = ctx.enter_context(nc.Block())

        def at(b, u, lag):
            db, uu = (u - lag) // UNITS, (u - lag) % UNITS
            bb = b + db
            if isinstance(bb, int) and not 0 <= bb < NB:
                return None
            return bb, uu

        def walk(eng, pre, tick):
            pre(0, 0)
            for b in range(2):
                for u in range(UNITS):
                    tick(b, u, b % 2)
            with eng.Fori(1, NB // 2 - 1) as i:
                for s in range(2):
                    for u in range(UNITS):
                        tick(2 * i + s, u, s)
            for b in range(NB - 2, NB):
                for u in range(UNITS):
                    tick(b, u, b % 2)
            for u in range(UNITS - 1):
                tick(NB, u, 0)

        @block.sync
        def _(sp):
            sp.dma_start(ident[:], d["ident"]).then_inc(s_const, 16)
            for c in range(4):
                w = NT // 4
                sp.dma_start(X[:, c * w:(c + 1) * w, :], x_view[:, c * w:(c + 1) * w, :]).then_inc(s_x, 16)
            sp.dma_start(woT[:], d["wo0T"].rearrange("(k p) e -> p k e", p=P)).then_inc(s_const, 16)
            sp.dma_start(bo_bc[:], d["L0_xattn_b_out"].rearrange("(a n) -> a n", a=1).to_broadcast([P, D])).then_inc(s_const, 16)

            def load(b, s):
                wait(sp, s_klo, b - 1)
                sp.dma_start(ctx_rows[s][:], ctx_view[:, b, :, :]).then_inc(s_ctx[s], 16)
                wait(sp, s_mb, b - 1)
                sp.dma_start(mask_int[s][:], mask_view[:, b, :, :]).then_inc(s_mask[s], 16)

            def load_half(e, s):
                wait(sp, s_wc, 3 * (2 * e + s - 1))
                if isinstance(e, int) and e == NE:
                    src = (d["L1_ffn_Wfc_s"].rearrange("(k p) f -> p k f", p=P) if s == 0 else
                           d["L1_ffn_Wproj_s"].rearrange("(j p) c -> p j c", p=P))
                else:
                    src = (d["L1_ffn_Wfc"][bass.ds(e, 1)].rearrange("o (k p) f -> p (o k) f", p=P) if s == 0 else
                           d["L1_ffn_Wproj"][bass.ds(e, 1)].rearrange("o (j p) c -> p (o j) c", p=P))
                sp.dma_start(w_in[s][:].rearrange("p (k f) -> p k f", k=src.shape[1]), src).then_inc(s_wi[s], 16)

            def store_half(e, s):
                sp.wait_ge(s_wc, 3 * (2 * e + s + 1))
                sp.dma_start(halves_dram[bass.ds(2 * e + s, 1)].rearrange("o p n -> p (o n)"),
                             w_cut[s][:].rearrange("p a n -> p (a n)")).then_inc(s_ws[s], 16)

            for b in range(2):
                load(b, b)
                load_half(0, b)
            with sp.Fori(1, NB // 2) as i:
                for s in range(2):
                    load(2 * i + s, s)
                    load_half(i, s)
                    store_half(i - 1, s)
            for e in range(NB // 2, NE + 1):
                for s in range(2):
                    load_half(e, s)
                    store_half(e - 1, s)
            for s in range(2):
                store_half(NE, s)
            for s in range(2):
                sp.wait_ge(s_ws[s], 16 * (NE + 1))

        @block.gpsimd
        def _(pool):
            pool.wait_ge(s_const, 48)
            pool.tensor_copy(ident16[:], ident[:]).then_inc(s_id16, 1)
            for s in range(2):
                ins = pool.memset(kT[s][:], 0.0)
            ins.then_inc(s_kzero, 1)

            def pre(b, s):
                b1 = b + 1
                pool.wait_ge(s_ctx[s], 8 * (b - s) + 16)
                wait_apart(pool, s_passed_p, s_PV, UNITS * (b - 1))
                pool.tensor_copy(k_split[s][:, :, :, 0, :], ctx_rows[s][:].rearrange("p t (h e) -> p t h e", h=H)).then_inc(s_khi, 1)
                pool.wait_ge(s_khi, b1)
                pool.tensor_tensor(k_split[s][:, :, :, 1, :], ctx_rows[s][:].rearrange("p t (h e) -> p t h e", h=H),
                                   k_split[s][:, :, :, 0, :], ALU.subtract).then_inc(s_klo, 1)
                wait_apart(pool, s_passed_p, s_klo, b1)
                pool.tensor_copy(k_split[s][:, :, :, 2:4, :].rearrange("p t h a e -> p (t h) (a e)"),
                                 k_split[s][:, :, :, 0:2, :].rearrange("p t h a e -> p (t h) (a e)")).then_inc(s_kdup, 1)
                pool.wait_ge(s_qn, b1)
                wait_apart(pool, s_passed_p, s_fillT, 4 * (b - 1))
                pool.tensor_copy(q_split[s][:, :, :, 0, :], q_rows[s][:].rearrange("p t (h e) -> p t h e", h=H)).then_inc(s_qhi, 1)
                for t in range(NQ):
                    ins = pool.tensor_tensor(X[:, NQ * b + t, :], X[:, NQ * b + t, :], bo_bc[:], ALU.add)
                ins.then_inc(s_bias, 1)
                pool.wait_ge(s_qhi, b1)
                pool.tensor_tensor(q_split[s][:, :, :, 2, :], q_rows[s][:].rearrange("p t (h e) -> p t h e", h=H),
                                   q_split[s][:, :, :, 0, :], ALU.subtract).then_inc(s_qlo, 1)
                wait_apart(pool, s_passed_p, s_qlo, b1)
                for t in range(NQ):
                    ins = pool.tensor_copy(q_split[s][:, t, :, 1:4:2, :], q_split[s][:, t, :, 0:3:2, :])
                ins.then_inc(s_qdup, 1)

            def cut(n, s):
                wait_apart(pool, s_passed_p, s_wi[s], 8 * (n - s) + 16)
                wait_apart(pool, s_passed_p, s_ws[s], 8 * (n - s))
                pool.tensor_scalar(w_in[s][:], w_in[s][:], WSCALE, None, ALU.mult).then_inc(s_wc, 1)
                wait_apart(pool, s_passed_p, s_wc, 3 * n + 1)
                pool.tensor_copy(w_cut[s][:, 0, :], w_in[s][:]).then_inc(s_wc, 1)
                pool.wait_ge(s_wc, 3 * n + 2)
                pool.tensor_tensor(w_cut[s][:, 1, :], w_in[s][:], w_cut[s][:, 0, :], ALU.subtract).then_inc(s_wc, 1)

            for b in range(2):
                pre(b, b)
                cut(b, b)
            with pool.Fori(1, NB // 2) as i:
                for s in range(2):
                    pre(2 * i + s, s)
                    cut(2 * i + s, s)
            for n in range(NB, 2 * (NE + 1)):
                cut(n, n % 2)

        @block.scalar
        def _(act):
            ln_scalar(act, ln, NT, 0)
            act.preload_act_table(ACT.Exp)

            def pre(b, s):
                pass

            def tick(b, u, s):
                w = at(b, u, 0)
                if w:
                    n = w[0] * UNITS + w[1]
                    p = u % 2
                    act.wait_ge(s_nm, n + 1)
                    wait(act, s_T, n - 1)
                    for j in range(2):
                        h = 2 * (u % HP) + j
                        ins = act.activation(probs[p][:, j, :], scores[p][:, j, :], ACT.Exp, bias=neg_max[p][:, j:j + 1],
                                             scale=SCALE, accum_out=row_sum[u // HP][:, h:h + 1])
                    ins.then_inc(s_exp, 1)
                w = at(b, u, 1)
                if w:
                    n = w[0] * UNITS + w[1]
                    p = w[1] % 2
                    act.wait_ge(s_T, n + 1)
                    wait(act, s_PV, n - 3)
                    act.activation(p_hi[w[1] % 4][:].rearrange("p a b c -> p (a b c)"), psum_t[p], ACT.Copy).then_inc(s_cast, 1)
                w = at(b, u, 5)
                if w and w[1] % HP == HP - 1:
                    m = w[0] * NQ + w[1] // HP
                    act.wait_ge(s_oTp, m + 1)
                    wait(act, s_op, m)
                    act.activation(oT[:].rearrange("p a b -> p (a b)"), psum_w[:, 0:2 * P], ACT.Copy).then_inc(s_oT, 1)

            walk(act, pre, tick)

        @block.tensor
        def _(pe):
            pe.wait_ge(s_const, 48)
            pe.wait_ge(s_id16, 1)
            pe.wait_ge(s_kzero, 1)

            def fill(b, f, s):
                src = (k_split if f < 2 else q_split)[s]
                pe.wait_ge(s_kdup if f < 2 else s_qdup, b + 1)
                wait(pe, s_fill, 4 * b + f)
                for hp in range(HP):
                    ins = pe.transpose(psum_fill.bitcast(F16)[:, hp * P:(hp + 1) * P],
                                       src[:, f % 2, 2 * hp:2 * hp + 2, :, :].rearrange("p h a e -> p (h a e)"), ident16[:])
                ins.then_inc(s_fillT, 1)

            def pre(b, s):
                for f in range(4):
                    fill(b, f, s)

            def tick(b, u, s):
                w = at(b, u, 0)
                if w:
                    n = w[0] * UNITS + w[1]
                    if u == 0:
                        pe.wait_ge(s_fill, 4 * w[0] + 4)
                    wait(pe, s_ttr, n - 1)
                    hp, t = u % HP, u // HP
                    for j in range(2):
                        ins = pe.matmul(psum_s[u % 2][:, j * S:(j + 1) * S], qT[s][:, hp, t * P:(t + 1) * P],
                                        kT[s][:, j, hp, :], start=True, stop=True)
                    ins.then_inc(s_S, 1)
                w = at(b, u, 1)
                if w:
                    n = w[0] * UNITS + w[1]
                    p = w[1] % 2
                    pe.wait_ge(s_exp, n + 1)
                    wait(pe, s_sub, n - 1)
                    for j in range(2):
                        for k in range(NQ):
                            ins = pe.transpose(psum_t[p][:, (NQ * j + k) * P:(NQ * j + k + 1) * P],
                                               probs[p][:, j, k * P:(k + 1) * P], ident[:])
                    ins.then_inc(s_T, 1)
                w = at(b, u, 3)
                if w:
                    n = w[0] * UNITS + w[1]
                    p, hp, t = w[1] % 2, w[1] % HP, w[1] // HP
                    sv = (s if u >= 3 else 1 - s)
                    pe.wait_ge(s_sub, n + 1)
                    if hp == 0:
                        wait(pe, s_on, NQ * (w[0] - 1) + t + 1)
                    for j in range(2):
                        h = 2 * hp + j
                        for i, (part, k) in enumerate([(q, k) for q in (p_hi, p_lo) for k in range(NQ)]):
                            ins = pe.matmul(psum_o[t][:, h * 2 * DH:(h + 1) * 2 * DH], part[w[1] % 4][:, j, k, :],
                                            k_split[sv][:, k, h, 0:2, :].rearrange("p a e -> p (a e)"),
                                            start=(i == 0), stop=(i == 2 * NQ - 1))
                    ins.then_inc(s_PV, 1)
                w = at(b, u, 5)
                if w and w[1] % HP == HP - 1:
                    m = w[0] * NQ + w[1] // HP
                    pe.wait_ge(s_on, m + 1)
                    wait(pe, s_xadd, m)
                    for k in range(2):
                        ins = pe.transpose(psum_w[:, k * P:(k + 1) * P], o_rows[w[1] // HP][:, k * P:(k + 1) * P], ident[:])
                    ins.then_inc(s_oTp, 1)
                w = at(b, u, 6)
                if w and w[1] % HP == HP - 1:
                    m = w[0] * NQ + w[1] // HP
                    pe.wait_ge(s_oT, m + 1)
                    for k in range(2):
                        ins = pe.matmul(psum_w[:, 2 * P:2 * P + D], oT[:, k, :], woT[:, k, :], start=(k == 0), stop=(k == 1))
                    ins.then_inc(s_op, 1)
                if u in (8, 10, 12, 14) and not (isinstance(b, int) and b + 1 >= NB):
                    fill(b + 1, (u - 8) // 2, 1 - s)

            walk(pe, pre, tick)

        @block.vector
        def _(v):
            v.wait_ge(s_x, 64)
            ln_vector(v, ln, X, NT, D, 0)

            def fill(b, f, s):
                v.wait_ge(s_fillT, 4 * b + f + 1)
                cols = slice((f % 2) * P, (f % 2 + 1) * P)
                src = psum_fill.bitcast(F16).rearrange("p (h q) -> p h q", h=HP)
                if f < 2:
                    for j in range(2):
                        rows = slice(SPLIT * j, SPLIT * j + SPLIT)
                        ins = v.tensor_copy(kT[s][rows, j, :, cols], src[rows, :, :])
                else:
                    ins = v.tensor_copy(qT[s][:, :, cols], src)
                ins.then_inc(s_fill, 1)

            def prepare(b, s):
                wait(v, s_qdup, b - 1)
                for t in range(NQ):
                    T = NQ * b + t
                    ins = v.tensor_scalar(q_rows[s][:, t, :], X[:, T, :], rstd[:, bass.ts(T, 1)], nmr[:, bass.ts(T, 1)], ALU.mult, ALU.add)
                ins.then_inc(s_qn, 1)
                v.wait_ge(s_mask[s], 8 * (b - s) + 16)
                v.tensor_scalar(mask_bias[s][:], mask_int[s][:], 0, -1e20, ALU.is_equal, ALU.mult).then_inc(s_mb, 1)

            def pre(b, s):
                prepare(b, s)
                v.wait_ge(s_kzero, 1)
                for f in range(4):
                    fill(b, f, s)

            def tick(b, u, s):
                more = not (isinstance(b, int) and b + 1 >= NB)
                if u == 0 and more:
                    prepare(b + 1, 1 - s)
                w = at(b, u, 0)
                if w:
                    n = w[0] * UNITS + w[1]
                    p = u % 2
                    v.wait_ge(s_S, n + 1)
                    if u == 0:
                        v.wait_ge(s_mb, w[0] + 1)
                    wait_apart(v, s_passed_v, s_exp, n - 1)
                    for j in range(2):
                        ins = v.tensor_tensor_reduce(scores[p][:, j, :], psum_s[p][:, j * S:(j + 1) * S], mask_bias[s][:, u // HP, :],
                                                     1.0, -3e38, ALU.add, ALU.max, row_max[p][:, j:j + 1])
                    ins.then_inc(s_ttr, 1)
                    v.wait_ge(s_ttr, n + 1)
                    v.tensor_scalar(neg_max[p][:], row_max[p][:], -SCALE, None, ALU.mult).then_inc(s_nm, 1)
                w = at(b, u, 2)
                if w:
                    n = w[0] * UNITS + w[1]
                    p = w[1] % 2
                    v.wait_ge(s_cast, n + 1)
                    v.tensor_tensor(p_lo[w[1] % 4][:].rearrange("p a b c -> p (a b c)"), psum_t[p],
                                    p_hi[w[1] % 4][:].rearrange("p a b c -> p (a b c)"), ALU.subtract).then_inc(s_sub, 1)
                w = at(b, u, 4)
                if w and w[1] % HP == HP - 1:
                    t = w[1] // HP
                    m = w[0] * NQ + t
                    v.wait_ge(s_PV, w[0] * UNITS + w[1] + 1)
                    v.reciprocal(row_rec[:], row_sum[t][:]).then_inc(s_rec, 1)
                    v.tensor_reduce(o_sum[:], psum_o[t].rearrange("p (h a e) -> p h e a", h=H, a=2), AX.X, ALU.add).then_inc(s_osum, 1)
                    v.wait_ge(s_rec, m + 1)
                    v.wait_ge(s_osum, m + 1)
                    v.tensor_tensor(o_rows[t][:].rearrange("p (h e) -> p h e", h=H), o_sum[:],
                                    row_rec[:].rearrange("p (h a) -> p h a", a=1).to_broadcast([P, H, DH]), ALU.mult).then_inc(s_on, 1)
                w = at(b, u, 7)
                if w and w[1] % HP == HP - 1:
                    m = w[0] * NQ + w[1] // HP
                    v.wait_ge(s_op, m + 1)
                    v.wait_ge(s_bias, w[0] + 1)
                    v.tensor_tensor(X[:, m, :], X[:, m, :], psum_w[:, 2 * P:2 * P + D], ALU.add).then_inc(s_xadd, 1)
                if u in (9, 11, 13, 15) and more:
                    fill(b + 1, (u - 9) // 2, 1 - s)

            walk(v, pre, tick)



ROUND = 1.5 * 2.0 ** 23
QEPS = 1e-8


def quant_mlp(nc, d, g, X, ident, banks):
    NT, D = g.NT, g.D
    FF = d["L0_ffn_w1"].shape[0]
    J = FF // P
    KC = D // P
    TPC = 4
    NC = NT // TPC
    CW = TPC * P

    with ExitStack() as ctx:
        def sb(name, shape, dt=F32):
            return ctx.enter_context(nc.sbuf_tensor(name, shape, dt))

        def sem(name):
            return ctx.enter_context(nc.semaphore(name))

        ln = g.ln
        xn = sb("xn", [P, NT, D])
        xq_tmp = [sb(f"xq_tmp{i}", [P, TPC, D]) for i in range(2)]
        xq = [sb(f"xq{i}", [P, TPC, D], BF16) for i in range(2)]
        xqT = sb("xqT", [P, KC, NT * P], BF16)
        w1 = sb("w1", [P, J, D])
        w2 = sb("w2", [P, KC, FF])
        w1q = sb("w1q", [P, J, D], BF16)
        w2q = sb("w2q", [P, KC, FF], BF16)
        w1T = sb("w1T", [P, KC, FF], BF16)
        w2T = sb("w2T", [P, J, D], BF16)
        b1 = sb("b1", [P, J])
        b2_bc = sb("b2_bc", [P, D])
        ident_bf = sb("ident_bf", [P, P], BF16)
        ones = sb("ones", [P, P])
        sw1 = sb("sw1", [P, J])
        sw2 = sb("sw2", [P, KC])
        rw1 = sb("rw1", [P, J])
        rw2 = sb("rw2", [P, KC])
        r_in = sb("r_in", [P, 1])
        r_h = sb("r_h", [P, 1])
        rscale1 = sb("rscale1", [P, J])
        rscale2 = sb("rscale2", [P, D])
        sw2_diag = sb("sw2_diag", [P, KC, P])
        sw2_bc = sb("sw2_bc", [P, D])
        scale1 = sb("scale1", [P, J])
        tmpj = sb("tmpj", [P, J])
        bq1 = sb("bq1", [P, J])
        scale2 = sb("scale2", [P, D])
        tmpd = sb("tmpd", [P, D])
        bq2 = sb("bq2", [P, D])
        part_max = sb("part_max", [P, 1])
        all_max = sb("all_max", [P, 1])
        s_in = sb("s_in", [P, 1])
        hidden_max = sb("hidden_max", [P, NC, J])
        hm = sb("hm", [P, J])
        h_part = sb("h_part", [P, 1])
        h_all = sb("h_all", [P, 1])
        s_h = sb("s_h", [P, 1])
        hf = [sb(f"hf{i}", [P, 2, CW]) for i in range(2)]
        hr = [sb(f"hr{i}", [P, 2, CW]) for i in range(2)]
        hq = [sb(f"hq{i}", [P, J, CW], BF16) for i in range(2)]
        y = [sb(f"y{i}", [P, TPC, D]) for i in range(2)]

        m_pass = g.passed_pool
        m_w = sem("weights_in")
        m_ib = sem("ident_bf_ready")
        m_v = sem("vector_step")
        m_wq = sem("weights_rounded")
        m_diag = sem("sw2_diag_ready")
        m_wt = sem("weights_transposed")
        m_wc = sem("weights_copied")
        m_bc = sem("sw2_spread")
        m_xn = sem("xn_ready")
        m_pm = sem("part_max_ready")
        m_am = sem("all_max_ready")
        m_a = sem("x_scaled")
        m_b = sem("x_rounded_up")
        m_q = sem("xq_ready")
        m_t = sem("xq_transposed")
        m_c = sem("xqT_ready")
        m_f = sem("hidden_for_max")
        m_m = sem("hidden_max_taken")
        m_hp = sem("h_part_ready")
        m_ha = sem("h_all_ready")
        m_sh = sem("s_h_ready")
        m_f2 = sem("hidden_in_psum")
        m_h = sem("hidden_relu")
        m_ha2 = sem("hidden_scaled")
        m_hq = sem("hq_ready")
        m_y = sem("output_in_psum")
        m_ys = sem("output_scaled")
        m_bq2 = sem("bq2_ready")
        m_xa = sem("x_added")
        m_xb = sem("x_bias_added")

        block = ctx.enter_context(nc.Block())

        @block.sync
        def _(sp):
            sp.dma_start(w1[:], d["L0_ffn_w1"].rearrange("(j p) c -> p j c", p=P)).then_inc(m_w, 16)
            sp.dma_start(w2[:], d["L0_ffn_w2"].rearrange("(k p) f -> p k f", p=P)).then_inc(m_w, 16)
            sp.dma_start(b1[:], d["ffn_b1"]).then_inc(m_w, 16)
            sp.dma_start(b2_bc[:], d["L0_ffn_b2"].rearrange("(a n) -> a n", a=1).to_broadcast([P, D])).then_inc(m_w, 16)
            sp.wait_ge(m_w, 64)

        @block.gpsimd
        def _(pool):
            pool.tensor_copy(ident_bf[:], ident[:]).then_inc(m_ib, 1)
            pool.wait_ge(m_ib, 1)
            pool.memset(ones[:], 1.0).then_inc(m_ib, 1)
            pool.wait_ge(m_pm, 1)
            pool.partition_all_reduce(all_max[:], part_max[:], P, bass.bass_isa.ReduceOp.max).then_inc(m_am, 1)
            pool.wait_ge(m_hp, 1)
            pool.partition_all_reduce(h_all[:], h_part[:], P, bass.bass_isa.ReduceOp.max).then_inc(m_ha, 1)
            pool.wait_ge(m_bq2, 1)

            def add(c, i):
                for t in range(TPC):
                    T = TPC * c + t
                    ins = pool.tensor_tensor(X[:, T, :], X[:, T, :], bq2[:], ALU.add)
                ins.then_inc(m_xb, 1)
                pool.wait_ge(m_xb, c + 1)
                wait_apart(pool, m_pass, m_ys, c + 1)
                for t in range(TPC):
                    T = TPC * c + t
                    ins = pool.tensor_tensor(X[:, T, :], X[:, T, :], y[i][:, t, :], ALU.add)
                ins.then_inc(m_xa, 1)

            with pool.Fori(0, NC // 2) as i:
                for s in range(2):
                    add(2 * i + s, s)

        @block.scalar
        def _(act):
            ln_scalar(act, ln, NT, 1)
            for k in range(4):
                act.wait_ge(m_wt, k + 1)
                src = banks[k // 2].bitcast(BF16)[:, (k % 2) * 1024:(k % 2) * 1024 + 1024]
                if k < 2:
                    act.activation(w1T[:, k, :], src, ACT.Copy).then_inc(m_wc, 1)
                else:
                    dst = w2T[:, 4 * (k - 2):4 * (k - 1), :].rearrange("p j c -> p (j c)")
                    act.activation(dst, src, ACT.Copy).then_inc(m_wc, 1)

            def columns(c, i):
                act.wait_ge(m_t, c + 1)
                src = banks[3].bitcast(BF16)[:, i * 1024:i * 1024 + 1024].rearrange("p (k t) -> p k t", k=KC)
                act.activation(xqT[:, :, bass.ts(c, CW)], src, ACT.Copy).then_inc(m_c, 1)

            with act.Fori(0, NC // 2) as n:
                for i in range(2):
                    columns(2 * n + i, i)

            act.wait_ge(m_sh, 1)

            def hidden(c, jp, first):
                n = c * (J // 2) + jp
                act.wait_ge(m_f2, n + 1)
                if not (first and jp < 2):
                    act.wait_ge(m_ha2, n - 1)
                for q in range(2):
                    j = 2 * jp + q
                    ins = act.activation(hf[jp % 2][:, q, :], banks[jp % 2][:, q * CW:(q + 1) * CW], ACT.Relu,
                                         bias=bq1[:, j:j + 1], scale=scale1[:, j:j + 1])
                ins.then_inc(m_h, 1)

            for jp in range(J // 2):
                hidden(0, jp, True)
            with act.Fori(1, NC) as c:
                for jp in range(J // 2):
                    hidden(c, jp, False)

        @block.tensor
        def _(pe):
            pe.wait_ge(m_ib, 2)
            for k in range(4):
                pe.wait_ge(m_wq, 1 if k < 2 else 2)
                dst = banks[k // 2].bitcast(BF16)[:, (k % 2) * 1024:(k % 2) * 1024 + 1024]
                for e in range(8):
                    if k < 2:
                        src = w1q[:, e, k * P:(k + 1) * P]
                    else:
                        j = 4 * (k - 2) + e // 2
                        src = w2q[:, e % 2, j * P:(j + 1) * P]
                    ins = pe.transpose(dst[:, e * P:(e + 1) * P], src, ident_bf[:])
                ins.then_inc(m_wt, 1)
            pe.wait_ge(m_diag, 1)
            for k in range(KC):
                ins = pe.matmul(banks[2][:, k * P:(k + 1) * P], ones[:], sw2_diag[:, k, :], start=True, stop=True)
            ins.then_inc(m_bc, 1)

            def columns(c, i, first):
                pe.wait_ge(m_q, c + 1)
                if not first:
                    pe.wait_ge(m_c, c - 1)
                for t in range(TPC):
                    for k in range(KC):
                        at = i * 1024 + k * CW + t * P
                        ins = pe.transpose(banks[3].bitcast(BF16)[:, at:at + P], xq[i][:, t, k * P:(k + 1) * P], ident_bf[:])
                ins.then_inc(m_t, 1)

            for i in range(2):
                columns(i, i, True)
            with pe.Fori(1, NC // 2) as n:
                for i in range(2):
                    columns(2 * n + i, i, False)

            pe.wait_ge(m_wc, 4)
            pe.wait_ge(m_c, NC)

            def first_linear(c, jp, done):
                for q in range(2):
                    j = 2 * jp + q
                    for k in range(KC):
                        ins = pe.matmul(banks[jp % 2][:, q * CW:(q + 1) * CW], w1T[:, k, j * P:(j + 1) * P],
                                        xqT[:, k, bass.ts(c, CW)], start=(k == 0), stop=(k == KC - 1))
                ins.then_inc(done, 1)

            def for_max(c, jp, first):
                if not (first and jp < 2):
                    pe.wait_ge(m_m, c * (J // 2) + jp - 1)
                first_linear(c, jp, m_f)

            for jp in range(J // 2):
                for_max(0, jp, True)
            with pe.Fori(1, NC) as c:
                for jp in range(J // 2):
                    for_max(c, jp, False)
            pe.wait_ge(m_m, NC * (J // 2))

            def second_linear(c, i, first):
                if not first:
                    pe.wait_ge(m_ys, c)
                pe.wait_ge(m_hq, c * (J // 2) + J // 2)
                for t in range(TPC):
                    for j in range(J):
                        ins = pe.matmul(banks[2][:, t * D:(t + 1) * D], hq[i][:, j, t * P:(t + 1) * P], w2T[:, j, :],
                                        start=(j == 0), stop=(j == J - 1))
                ins.then_inc(m_y, 1)

            def values(c, i, first):
                for jp in range(J // 2):
                    if not (first and jp < 2):
                        pe.wait_ge(m_h, c * (J // 2) + jp - 1)
                    first_linear(c, jp, m_f2)

            values(0, 0, True)
            values(1, 1, False)
            second_linear(0, 0, True)
            with pe.Fori(1, NC // 2) as n:
                values(2 * n, 0, False)
                second_linear(2 * n - 1, 1, False)
                values(2 * n + 1, 1, False)
                second_linear(2 * n, 0, False)
            second_linear(NC - 1, 1, False)

        @block.vector
        def _(v):
            done = 0

            def link(ins):
                nonlocal done
                ins.then_inc(m_v, 1)
                done += 1
                v.wait_ge(m_v, done)

            v.wait_ge(m_w, 64)
            link(v.tensor_reduce(sw1[:], w1[:], AX.X, ALU.max, apply_absolute_value=True))
            link(v.tensor_reduce(sw2[:], w2[:], AX.X, ALU.max, apply_absolute_value=True))
            link(v.tensor_scalar(sw1[:], sw1[:], QEPS, 1 / 127.0, ALU.max, ALU.mult))
            link(v.tensor_scalar(sw2[:], sw2[:], QEPS, 1 / 127.0, ALU.max, ALU.mult))
            link(v.reciprocal(rw1[:], sw1[:]))
            link(v.reciprocal(rw2[:], sw2[:]))
            for j in range(J):
                ins = v.tensor_scalar(w1[:, j, :], w1[:, j, :], rw1[:, j:j + 1], 127.0, ALU.mult, ALU.min)
            for k in range(KC):
                ins = v.tensor_scalar(w2[:, k, :], w2[:, k, :], rw2[:, k:k + 1], 127.0, ALU.mult, ALU.min)
            link(ins)
            link(v.tensor_scalar(w1[:], w1[:], -128.0, ROUND, ALU.max, ALU.add))
            v.tensor_scalar(w1q[:], w1[:], ROUND, None, ALU.subtract).then_inc(m_wq, 1)
            link(v.tensor_scalar(w2[:], w2[:], -128.0, ROUND, ALU.max, ALU.add))
            v.tensor_scalar(w2q[:], w2[:], ROUND, None, ALU.subtract).then_inc(m_wq, 1)
            v.wait_ge(m_ib, 2)
            for k in range(KC):
                ins = v.tensor_scalar(sw2_diag[:, k, :], ident[:], sw2[:, k:k + 1], None, ALU.mult)
            ins.then_inc(m_diag, 1)

            ln_vector(v, ln, X, NT, D, 1)
            with v.Fori(0, NT) as T:
                v.tensor_scalar(xn[:, T, :], X[:, T, :], ln["rstd"][:, bass.ts(T, 1)], ln["nmr"][:, bass.ts(T, 1)],
                                ALU.mult, ALU.add).then_inc(m_xn, 1)
            v.wait_ge(m_bc, 1)
            v.tensor_copy(sw2_bc[:], banks[2][:, 0:D]).then_inc(m_v, 1)
            done += 1
            v.wait_ge(m_xn, NT)
            v.tensor_reduce(part_max[:], xn[:], AX.XY, ALU.max).then_inc(m_pm, 1)
            v.wait_ge(m_am, 1)
            link(v.tensor_scalar(s_in[:], all_max[:], QEPS, 1 / 255.0, ALU.max, ALU.mult))
            link(v.reciprocal(r_in[:], s_in[:]))

            def quantise(c, i, first):
                at = slice(TPC * c, TPC * c + TPC) if isinstance(c, int) else bass.ts(c, TPC)
                v.tensor_scalar(xq_tmp[i][:], xn[:, at, :], r_in[:, 0:1], 0.0, ALU.mult, ALU.max).then_inc(m_a, 1)
                v.wait_ge(m_a, c + 1)
                v.tensor_scalar(xq_tmp[i][:], xq_tmp[i][:], 255.0, ROUND, ALU.min, ALU.add).then_inc(m_b, 1)
                v.wait_ge(m_b, c + 1)
                if not first:
                    v.wait_ge(m_t, c - 1)
                v.tensor_scalar(xq[i][:], xq_tmp[i][:], ROUND, None, ALU.subtract).then_inc(m_q, 1)

            for i in range(2):
                quantise(i, i, True)
            with v.Fori(1, NC // 2) as n:
                for i in range(2):
                    quantise(2 * n + i, i, False)

            link(v.tensor_scalar(scale1[:], sw1[:], s_in[:, 0:1], None, ALU.mult))
            link(v.reciprocal(rscale1[:], scale1[:]))
            link(v.tensor_tensor(tmpj[:], b1[:], rscale1[:], ALU.mult))
            link(v.tensor_scalar(tmpj[:], tmpj[:], ROUND, None, ALU.add))
            link(v.tensor_scalar(tmpj[:], tmpj[:], ROUND, None, ALU.subtract))
            link(v.tensor_tensor(bq1[:], tmpj[:], scale1[:], ALU.mult))

            with v.Fori(0, NC) as c:
                for jp in range(J // 2):
                    v.wait_ge(m_f, c * (J // 2) + jp + 1)
                    v.tensor_reduce(hidden_max[:, c, 2 * jp:2 * jp + 2], banks[jp % 2][:].rearrange("p (q t) -> p q t", q=2),
                                    AX.X, ALU.max).then_inc(m_m, 1)
            v.wait_ge(m_m, NC * (J // 2))
            link(v.tensor_reduce(hm[:], hidden_max[:].rearrange("p c j -> p j c"), AX.X, ALU.max))
            link(v.tensor_tensor(hm[:], hm[:], scale1[:], ALU.mult))
            link(v.tensor_tensor(hm[:], hm[:], bq1[:], ALU.add))
            link(v.tensor_reduce(h_part[:], hm[:], AX.X, ALU.max))
            v.tensor_scalar(h_part[:], h_part[:], 0.0, None, ALU.max).then_inc(m_hp, 1)
            v.wait_ge(m_ha, 1)
            v.tensor_scalar(s_h[:], h_all[:], QEPS, 1 / 255.0, ALU.max, ALU.mult).then_inc(m_sh, 1)
            v.wait_ge(m_sh, 1)
            link(v.reciprocal(r_h[:], s_h[:]))
            link(v.tensor_scalar(scale2[:], sw2_bc[:], s_h[:, 0:1], None, ALU.mult))
            link(v.reciprocal(rscale2[:], scale2[:]))
            link(v.tensor_tensor(tmpd[:], b2_bc[:], rscale2[:], ALU.mult))
            link(v.tensor_scalar(tmpd[:], tmpd[:], ROUND, None, ALU.add))
            link(v.tensor_scalar(tmpd[:], tmpd[:], ROUND, None, ALU.subtract))
            v.tensor_tensor(bq2[:], tmpd[:], scale2[:], ALU.mult).then_inc(m_bq2, 1)

            def hidden(c, i, first):
                for jp in range(J // 2):
                    n = c * (J // 2) + jp
                    v.wait_ge(m_h, n + 1)
                    v.tensor_scalar(hr[jp % 2][:], hf[jp % 2][:], r_h[:, 0:1], 255.0, ALU.mult, ALU.min).then_inc(m_ha2, 1)
                    v.wait_ge(m_ha2, n + 1)
                    if jp == 0 and not first:
                        v.wait_ge(m_y, c - 1)
                    v.tensor_scalar(hq[i][:, 2 * jp:2 * jp + 2, :], hr[jp % 2][:], ROUND, ROUND, ALU.add, ALU.subtract)\
                     .then_inc(m_hq, 1)

            def output(c, i, first):
                v.wait_ge(m_y, c + 1)
                if not first:
                    v.wait_ge(m_xa, c - 1)
                v.tensor_tensor(y[i][:], banks[2][:].rearrange("p (t c) -> p t c", t=TPC),
                                scale2[:].rearrange("p (t c) -> p t c", t=1).to_broadcast([P, TPC, D]), ALU.mult).then_inc(m_ys, 1)

            hidden(0, 0, True)
            hidden(1, 1, True)
            output(0, 0, True)
            hidden(2, 0, False)
            output(1, 1, True)
            hidden(3, 1, False)
            output(2, 0, False)
            with v.Fori(2, NC // 2) as n:
                hidden(2 * n, 0, False)
                output(2 * n - 1, 1, False)
                hidden(2 * n + 1, 1, False)
                output(2 * n, 0, False)
            output(NC - 1, 1, False)


def autocorrelation(nc, d, g, X, ident, banks):
    NB, S, D, NQ, NT = g.NB, g.S, g.D, g.NQ, g.NT
    KC = D // P
    DZ = D + 1
    TOPK = 6
    BIG = 1e30

    with ExitStack() as ctx:
        def sb(name, shape, dt=F32):
            return ctx.enter_context(nc.sbuf_tensor(name, shape, dt))

        def sem(name):
            return ctx.enter_context(nc.semaphore(name))

        ln = g.ln
        wkT = sb("wkT", [P, KC, D])
        wqTb = sb("wqTb", [P, KC, DZ])
        wvT = sb("wvT", [P, KC, D])
        wo = sb("wo", [P, KC, D])
        bk = sb("bk", [P, KC])
        bv = sb("bv", [P, KC])
        bv_wide = sb("bv_wide", [P, KC, P])
        bo2_bc = sb("bo2_bc", [P, D])
        wz = sb("wz", [P, KC, DZ])
        wv_o = sb("wv_o", [P, KC, D])
        bias_bc = sb("bias_bc", [P, D])
        zf_bias = sb("zf_bias", [P, NQ, DZ])
        dft = sb("dft", [P, NQ, S])
        flip = sb("flip", [P, P])
        dft_flipped = sb("dft_flipped", [P, NQ, S])
        idft = sb("idft", [P, 3, S])
        lag_rank = sb("lag_rank", [NB, S])
        dc = sb("dc", [P, 1])
        ctx_in = [sb(f"c_rows{s}", [P, NQ, D]) for s in range(2)]
        ctxT = [sb(f"c_T{s}", [P, KC, S]) for s in range(2)]
        z = [sb(f"z{s}", [P, NQ, DZ]) for s in range(2)]
        zf = sb("zf", [P, NB, NQ, DZ])
        vp = sb("vp", [P, NT, D])
        xr = [sb(f"x_rows{s}", [P, NQ, D]) for s in range(2)]
        prod = [sb(f"prod{s}", [P, 4, D]) for s in range(2)]
        sums = sb("sums", [P, NB, 4])
        freq = sb("freq", [P, 3, NB])
        corr = sb("corr", [NB, S])
        mean16 = sb("mean16", [NB, NB])
        work = sb("work", [NB, S])
        cand = sb("cand", [NB, S])
        hot = sb("hot", [NB, S])
        sel = sb("sel", [NB, S])
        peak = sb("peak", [NB, 1])
        first = sb("first", [NB, 1])
        top = sb("top", [NB, 1])
        total = sb("total", [NB, 1])
        lag_w = sb("lag_w", [NB, 2, S])
        lag_e = sb("lag_e", [NB, S])
        mixT = sb("mixT", [P, NB, NQ, S])
        lag_dram = nc.dram_tensor("lag_weights", [NB, 2 * S], F32).ap()

        c_w = sem("c_weights_in")
        c_ctx = [sem(f"c_ctx_in{s}") for s in range(2)]
        c_set = sem("c_constants_set")
        c_wp = sem("c_weight_products")
        c_wr = sem("c_products_copied")
        c_v = sem("c_vector_step")
        c_tr = sem("ctx_transposed")
        c_cT = sem("ctxT_copied")
        c_pr = sem("ctx_projected")
        c_z = sem("z_copied")
        c_vp = sem("vp_copied")
        c_df = sem("z_frequencies")
        c_zf = sem("zf_copied")
        c_xr = sem("x_rows_ready")
        c_xf = sem("x_frequencies")
        c_pd = sem("products_ready")
        c_sm = sem("sums_ready")
        c_fr = sem("freq_ready")
        c_cr = sem("corr_in_psum")
        c_cc = sem("corr_copied")
        c_me = sem("mean_in_psum")
        c_tp = sem("top_ready")
        c_ex = sem("lag_exp_ready")
        c_lw = sem("lag_weights_ready")
        c_ls = sem("lag_weights_stored")
        c_mx = [sem(f"mixT_in{q}") for q in range(4)]
        c_mo = sem("mixed_in_psum")
        c_xa = sem("c_x_added")
        c_xb = sem("c_x_bias_added")

        block = ctx.enter_context(nc.Block())
        rows = d["ctx_1024"].rearrange("b (t p) c -> p b t c", p=P)

        def walk(eng, tick):
            for b in range(2):
                tick(b, b)
            with eng.Fori(1, NB // 2 - 1) as i:
                for s in range(2):
                    tick(2 * i + s, s)
            for b in range(NB - 2, NB + 1):
                tick(b, b % 2)

        def known(b):
            return isinstance(b, int)

        @block.sync
        def _(sp):
            for dst, src in ((wkT, d["wkT"]), (wvT, d["wvT"]), (wo, d["L1_xattn_Wo"])):
                sp.dma_start(dst[:], src.rearrange("(k p) e -> p k e", p=P)).then_inc(c_w, 16)
            sp.dma_start(wqTb[:], d["wqTb"].rearrange("(k p) e -> p k e", p=P)).then_inc(c_w, 16)
            sp.dma_start(bk[:], d["bk"]).then_inc(c_w, 16)
            sp.dma_start(bv[:], d["bv"]).then_inc(c_w, 16)
            sp.dma_start(bo2_bc[:], d["L1_xattn_bo"].rearrange("(a n) -> a n", a=1).to_broadcast([P, D])).then_inc(c_w, 16)
            sp.dma_start(dft[:], d["dft"].rearrange("(k p) f -> p k f", p=P)).then_inc(c_w, 16)
            sp.dma_start(idft[:], d["idft"].rearrange("(k p) f -> p k f", p=P)).then_inc(c_w, 16)
            sp.dma_start(dft_flipped[:], d["dft_flipped"].rearrange("(k p) f -> p k f", p=P)).then_inc(c_w, 16)
            sp.dma_start(flip[:], d["flip"]).then_inc(c_w, 16)
            sp.dma_start(lag_rank[:], d["lag_rank"]).then_inc(c_w, 16)
            sp.dma_start(dc[:], d["dc"]).then_inc(c_w, 16)

            def load(b, s):
                wait(sp, c_tr, b - 1)
                sp.dma_start(ctx_in[s][:], rows[:, b, :, :]).then_inc(c_ctx[s], 16)

            for b in range(2):
                load(b, b)
            with sp.Fori(1, NB // 2) as i:
                for s in range(2):
                    load(2 * i + s, s)
            sp.wait_ge(c_lw, 2)
            sp.dma_start(lag_dram, lag_w[:].rearrange("b a s -> b (a s)")).then_inc(c_ls, 16)
            sp.wait_ge(c_ls, 16)
            for q in range(4):
                for k in range(NQ):
                    n = NB // 4
                    src = bass.AP(tensor=lag_dram.tensor, offset=q * n * 2 * S + S - P - k * P, ap=[[1, P], [2 * S, n], [1, S]])
                    sp.dma_start(mixT[:, q * n:(q + 1) * n, k, :], src).then_inc(c_mx[q], 16)
            for q in range(4):
                sp.wait_ge(c_mx[q], 32)

        @block.gpsimd
        def _(pool):
            pool.memset(zf_bias[:], 0.0).then_inc(c_set, 1)
            pool.wait_ge(c_set, 1)
            pool.memset(mean16[:], 1.0 / NB).then_inc(c_set, 1)
            pool.wait_ge(c_set, 2)
            pool.memset(sel[:], 0.0).then_inc(c_set, 1)
            pool.wait_ge(c_wr, 4)
            pool.wait_ge(c_sm, NB)
            with pool.Fori(0, NT) as T:
                pool.tensor_tensor(X[:, T, :], X[:, T, :], bias_bc[:], ALU.add).then_inc(c_xb, 1)

        @block.scalar
        def _(act):
            def tick(b, s):
                if not (known(b) and b + 1 >= NB):
                    columns(b + 1, 1 - s)
                if not (known(b) and b >= NB):
                    act.wait_ge(c_pr, b + 1)
                    wait(act, c_df, b - 1)
                    act.activation(z[s][:], banks[1][:].rearrange("p (t c) -> p t c", t=NQ)[:, :, 0:DZ], ACT.Copy).then_inc(c_z, 1)
                    act.activation(vp[:, bass.ts(b, NQ), :], banks[2][:].rearrange("p (t c) -> p t c", t=NQ)[:, :, 0:D],
                                   ACT.Copy).then_inc(c_vp, 1)

            def columns(b, s):
                act.wait_ge(c_tr, b + 1)
                wait(act, c_pr, b - 1)
                act.activation(ctxT[s][:].rearrange("p k t -> p (k t)"), banks[0][:, s * 512:(s + 1) * 512], ACT.Copy).then_inc(c_cT, 1)

            columns(0, 0)
            walk(act, tick)
            ln_scalar(act, ln, NT, 2)
            act.wait_ge(c_tp, 1)
            act.activation(lag_e[:], work[:], ACT.Exp, bias=top[:, 0:1], scale=1.0, accum_out=total[:]).then_inc(c_ex, 1)

        @block.tensor
        def _(pe):
            pe.wait_ge(c_w, 16 * 13)
            for k in range(KC):
                for e in range(KC):
                    pe.matmul(banks[0][:, k * 512:k * 512 + DZ], wkT[:, e, k * P:(k + 1) * P], wqTb[:, e, :],
                              start=(e == 0), stop=(e == KC - 1))
            for k in range(KC):
                for e in range(KC):
                    ins = pe.matmul(banks[1][:, k * 512:k * 512 + D], wvT[:, e, k * P:(k + 1) * P], wo[:, e, :],
                                    start=(e == 0), stop=(e == KC - 1))
            for e in range(KC):
                pe.matmul(banks[2][0:1, 0:DZ], bk[:, e:e + 1], wqTb[:, e, :], start=(e == 0), stop=(e == KC - 1))
            pe.wait_ge(c_v, 1)
            for e in range(KC):
                ins = pe.matmul(banks[3][:, 0:D], bv_wide[:, e, :], wo[:, e, :], start=(e == 0), stop=(e == KC - 1))
            ins.then_inc(c_wp, 1)
            pe.wait_ge(c_wr, 4)

            def transposes(b, s):
                pe.wait_ge(c_ctx[s], 8 * (b - s) + 16)
                wait(pe, c_cT, b - 1)
                for k in range(KC):
                    for t in range(NQ):
                        at = s * 512 + k * S + t * P
                        ins = pe.transpose(banks[0][:, at:at + P], ctx_in[s][:, t, k * P:(k + 1) * P], flip[:])
                ins.then_inc(c_tr, 1)

            def tick(b, s):
                if not (known(b) and b + 1 >= NB):
                    transposes(b + 1, 1 - s)
                if not (known(b) and b >= NB):
                    pe.wait_ge(c_cT, b + 1)
                    wait(pe, c_vp, b)
                    for t in range(NQ):
                        for dst, w, n in ((banks[1], wz, DZ), (banks[2], wv_o, D)):
                            for k in range(KC):
                                ins = pe.matmul(dst[:, t * 512:t * 512 + n], ctxT[s][:, k, t * P:(t + 1) * P], w[:, k, :],
                                                start=(k == 0), stop=(k == KC - 1))
                    ins.then_inc(c_pr, 1)
                if not (known(b) and b < 1):
                    pe.wait_ge(c_z, b)
                    wait(pe, c_zf, b - 1)
                    for j in range(NQ):
                        for t in range(NQ):
                            ins = pe.matmul(banks[3][:, j * 512:j * 512 + DZ], dft_flipped[:, t, j * P:(j + 1) * P], z[1 - s][:, t, :],
                                            start=(t == 0), stop=(t == NQ - 1))
                    ins.then_inc(c_df, 1)

            transposes(0, 0)
            walk(pe, tick)

            def x_frequencies(b, s):
                pe.wait_ge(c_xr, b + 1)
                wait(pe, c_pd, b - 1)
                for j in range(NQ):
                    for t in range(NQ):
                        ins = pe.matmul(banks[s][:, j * D:(j + 1) * D], dft[:, t, j * P:(j + 1) * P], xr[s][:, t, :],
                                        start=(t == 0), stop=(t == NQ - 1))
                ins.then_inc(c_xf, 1)

            pe.wait_ge(c_vp, NB)
            for b in range(2):
                x_frequencies(b, b)
            with pe.Fori(1, NB // 2) as i:
                for s in range(2):
                    x_frequencies(2 * i + s, s)
            pe.wait_ge(c_fr, 1)
            for k in range(3):
                ins = pe.matmul(banks[2][0:NB, 0:S], freq[:, k, :], idft[:, k, :], start=(k == 0), stop=(k == 2))
            ins.then_inc(c_cr, 1)
            pe.wait_ge(c_cc, 1)
            pe.matmul(banks[2][0:NB, 512:512 + S], mean16[:], corr[:], start=True, stop=True).then_inc(c_me, 1)
            for b in range(NB):
                if b % (NB // 4) == 0:
                    pe.wait_ge(c_mx[b // (NB // 4)], 32)
                for l in range(NQ):
                    T = NQ * b + l
                    wait(pe, c_xa, T - 3)
                    for k in range(NQ):
                        ins = pe.matmul(banks[T % 4][:, 0:D], mixT[:, b, k, l * P:(l + 1) * P], vp[:, NQ * b + k, :],
                                        start=(k == 0), stop=(k == NQ - 1))
                    ins.then_inc(c_mo, 1)

        @block.vector
        def _(v):
            v.wait_ge(c_w, 16 * 13)
            for e in range(KC):
                ins = v.tensor_copy(bv_wide[:, e, :], bv[:, e:e + 1].to_broadcast([P, P]))
            ins.then_inc(c_v, 1)
            v.wait_ge(c_set, 3)
            v.wait_ge(c_wp, 1)
            halves = [banks[i][:].rearrange("p (k c) -> p k c", k=KC) for i in range(2)]
            v.tensor_copy(wz[:], halves[0][:, :, 0:DZ]).then_inc(c_wr, 1)
            v.tensor_copy(wv_o[:], halves[1][:, :, 0:D]).then_inc(c_wr, 1)
            v.tensor_scalar(zf_bias[0:1, 0, :], banks[2][0:1, 0:DZ], float(S), None, ALU.mult).then_inc(c_wr, 1)
            v.tensor_tensor(bias_bc[:], banks[3][:, 0:D], bo2_bc[:], ALU.add).then_inc(c_wr, 1)
            v.wait_ge(c_wr, 4)

            def copy_zf(b):
                v.wait_ge(c_df, b + 1)
                v.tensor_tensor(zf[:, b, :, :], banks[3][:].rearrange("p (t c) -> p t c", t=NQ)[:, :, 0:DZ], zf_bias[:], ALU.add)\
                 .then_inc(c_zf, 1)

            with v.Fori(0, NB) as b:
                copy_zf(b)
            ln_vector(v, ln, X, NT, D, 2)

            def normalised(b, s):
                wait(v, c_xf, b - 1)
                for t in range(NQ):
                    T = NQ * b + t
                    ins = v.tensor_scalar(xr[s][:, t, :], X[:, T, :], ln["rstd"][:, bass.ts(T, 1)], ln["nmr"][:, bass.ts(T, 1)],
                                          ALU.mult, ALU.add)
                ins.then_inc(c_xr, 1)

            def products(b, s):
                v.wait_ge(c_xf, b + 1)
                wait(v, c_sm, b - 1)
                xf = banks[s][:, 0:NQ * D].rearrange("p (j c) -> p j c", j=NQ)
                v.tensor_tensor(prod[s][:, 0:2, :], xf, zf[:, b, :, 0:D], ALU.mult)
                v.tensor_tensor(prod[s][:, 2, :], xf[:, 0, :], zf[:, b, 1, 0:D], ALU.mult)
                v.tensor_tensor(prod[s][:, 3, :], xf[:, 1, :], zf[:, b, 0, 0:D], ALU.mult).then_inc(c_pd, 1)
                v.wait_ge(c_pd, b + 1)
                v.tensor_reduce(sums[:, b, :], prod[s][:], AX.X, ALU.add).then_inc(c_sm, 1)

            v.wait_ge(c_zf, NB)
            normalised(0, 0)
            normalised(1, 1)
            products(0, 0)
            with v.Fori(1, NB // 2) as i:
                normalised(2 * i, 0)
                products(2 * i - 1, 1)
                normalised(2 * i + 1, 1)
                products(2 * i, 0)
            products(NB - 1, 1)
            v.wait_ge(c_sm, NB)

            done = 1

            def link(ins):
                nonlocal done
                ins.then_inc(c_v, 1)
                done += 1
                v.wait_ge(c_v, done)

            link(v.tensor_scalar(freq[:, 0, :], zf[:, :, 0, D], dc[:, 0:1], None, ALU.mult))
            link(v.tensor_tensor(freq[:, 0, :], freq[:, 0, :], sums[:, :, 0], ALU.add))
            link(v.tensor_copy(freq[:, 1, :], sums[:, :, 1]))
            v.tensor_tensor(freq[:, 2, :], sums[:, :, 3], sums[:, :, 2], ALU.subtract).then_inc(c_fr, 1)
            v.wait_ge(c_cr, 1)
            v.tensor_copy(corr[:], banks[2][0:NB, 0:S]).then_inc(c_cc, 1)
            v.wait_ge(c_me, 1)
            link(v.tensor_copy(work[:], banks[2][0:NB, 512:512 + S]))
            for k in range(TOPK):
                link(v.tensor_reduce(peak[:], work[:], AX.X, ALU.max))
                link(v.scalar_tensor_tensor(cand[:], work[:], peak[:, 0:1], lag_rank[:], ALU.is_equal, ALU.mult))
                link(v.tensor_reduce(first[:], cand[:], AX.X, ALU.max))
                link(v.tensor_scalar(hot[:], lag_rank[:], first[:, 0:1], None, ALU.is_equal))
                link(v.tensor_tensor(sel[:], sel[:], hot[:], ALU.add))
                link(v.scalar_tensor_tensor(work[:], hot[:], -3e38, work[:], ALU.mult, ALU.add))
            link(v.tensor_scalar(cand[:], sel[:], BIG, BIG, ALU.mult, ALU.subtract))
            link(v.tensor_tensor(work[:], corr[:], cand[:], ALU.add))
            link(v.tensor_reduce(peak[:], work[:], AX.X, ALU.max))
            v.tensor_scalar(top[:], peak[:], -1.0, None, ALU.mult).then_inc(c_tp, 1)
            v.wait_ge(c_ex, 1)
            link(v.reciprocal(first[:], total[:]))
            for k in range(2):
                v.tensor_scalar(lag_w[:, k, :], lag_e[:], first[:, 0:1], None, ALU.mult).then_inc(c_lw, 1)

            v.wait_ge(c_xb, NT)
            with v.Fori(0, NT // 4) as i:
                for q in range(4):
                    T = 4 * i + q
                    v.wait_ge(c_mo, T + 1)
                    v.tensor_tensor(X[:, T, :], X[:, T, :], banks[q][:, 0:D], ALU.add).then_inc(c_xa, 1)


def moe(nc, d, g, X, ident, banks, halves_dram):
    NB, S, D, NQ, NT = g.NB, g.S, g.D, g.NQ, g.NT
    NE, _, F = d["L1_ffn_Wfc"].shape
    KC, J = D // P, F // P
    SLOT = 256
    ST = SLOT // P
    PICKS = 2
    NSLOT = (PICKS * NT * P + NE * (SLOT - 1)) // SLOT
    MOST = NT * P // SLOT
    TPC = 4
    CHUNKS = NT // ST
    RING = 8
    EARLY = CHUNKS // 2
    LATE = CHUNKS - EARLY

    with ExitStack() as ctx:
        def sb(name, shape, dt=F32):
            return ctx.enter_context(nc.sbuf_tensor(name, shape, dt))

        def sem(name):
            return ctx.enter_context(nc.semaphore(name))

        slots_x = nc.dram_tensor("slots_x", [NSLOT * SLOT, D], F32).ap()
        slots_y = nc.dram_tensor("slots_y", [NSLOT * SLOT, D], F32).ap()

        ln = g.ln
        xn = sb("moe_xn", [P, NT, D])
        xT32 = [sb(f"moe_xT32_{i}", [P, KC, 4 * P]) for i in range(2)]
        xnT = sb("moe_xnT", [P, 2, KC, NT * P], F16)
        zeros = sb("zeros", [P, D])
        wr = sb("wr", [P, KC, NE])
        before = sb("before", [P, P])
        ones = sb("moe_ones", [P, P])
        e_rank = sb("e_rank", [P, NE])
        e_table = sb("e_table", [P, NE, MOST])
        s_table = sb("s_table", [P, NSLOT, NE])
        lT = [sb(f"lT{i}", [NE, 4 * P]) for i in range(2)]
        logit = sb("logit", [P, NT, NE])
        hot = [sb(f"hot{i}", [P, NT, NE]) for i in range(PICKS)]
        tmp = sb("moe_tmp", [P, NT, NE])
        tot = [sb(f"tot{i}", [P, NT, NE]) for i in range(2)]
        total = sb("moe_total", [P, NT, NE])
        base = sb("moe_base", [P, NT, NE])
        peak = [sb(f"moe_peak{i}", [P, NT]) for i in range(PICKS)]
        pick = sb("moe_pick", [P, NT])
        gate = [sb(f"gate{i}", [P, NT]) for i in range(PICKS)]
        posf = [sb(f"posf{i}", [P, NT]) for i in range(PICKS)]
        pos = [sb(f"pos{i}", [P, NT], I32) for i in range(PICKS)]
        cmp_e = sb("cmp_e", [P, NE, MOST])
        n_slots = sb("n_slots", [P, NE])
        start = sb("start", [P, NE + 1])
        cmp_s = sb("cmp_s", [P, NSLOT, NE])
        slot_ef = sb("slot_ef", [P, NSLOT])
        slot_e = sb("slot_e", [P, NSLOT], I32)

        w1 = [sb(f"moe_w1_{i}", [P, 2, KC, F], F16) for i in range(2)]
        w2 = [sb(f"moe_w2_{i}", [P, 2, J, D], F16) for i in range(2)]
        b1 = [sb(f"moe_b1_{i}", [P, J]) for i in range(2)]
        b2 = [sb(f"moe_b2_{i}", [P, D]) for i in range(2)]
        rows = [sb(f"moe_rows{i}", [P, ST, D]) for i in range(2)]
        rT = [sb(f"moe_rT{i}", [P, 2, KC, SLOT], F16) for i in range(2)]
        hf = [sb(f"moe_hf{i}", [P, J, SLOT]) for i in range(2)]
        hT = [sb(f"moe_hT{i}", [P, 2, J, SLOT], F16) for i in range(2)]
        y = [sb(f"moe_y{i}", [P, ST, D]) for i in range(2)]
        ring = [xn[:, i, :] for i in range(RING)]

        e_c = sem("moe_constants_in")
        e_set = sem("moe_constants_set")
        e_zero = sem("slots_zeroed")
        e_v = sem("moe_vector_step")
        e_xn = sem("moe_xn_ready")
        e_t = sem("moe_xn_transposed")
        e_tc = sem("moe_xT32_copied")
        e_xh = sem("moe_xnT_high")
        e_xl = sem("moe_xnT_low")
        e_l = sem("logits_in_psum")
        e_lc = sem("logits_copied")
        e_lt = sem("logits_transposed")
        e_d = sem("gate_difference")
        e_e = sem("gate_exp_ready")
        e_m = sem("picks_ready")
        e_p = sem("prefix_in_psum")
        e_pos = sem("positions_ready")
        e_slot = sem("slot_experts_ready")
        e_sc = sem("rows_scattered")
        e_w1 = [sem(f"moe_w1_in{i}") for i in range(2)]
        e_w2 = [sem(f"moe_w2_in{i}") for i in range(2)]
        e_r = [sem(f"moe_rows_in{i}") for i in range(2)]
        e_rt = sem("rows_transposed")
        e_rh = sem("rT_high")
        e_rl = sem("rT_low")
        e_f = sem("moe_hidden_in_psum")
        e_g = sem("moe_gelu_done")
        e_hh = sem("moe_hidden_high")
        e_hl = sem("moe_hidden_low")
        e_o = sem("moe_output_in_psum")
        e_y = sem("moe_output_taken")
        e_st = [sem(f"moe_y_stored{i}") for i in range(2)]
        e_ga = [sem(f"rows_gathered{i}") for i in range(RING)]
        e_ad = sem("gathered_added")
        e_b = sem("shared_bias_added")

        block = ctx.enter_context(nc.Block())

        def walk(eng, tick):
            for s in range(2):
                tick(s, s)
            with eng.Fori(1, NSLOT // 2) as i:
                for p in range(2):
                    tick(2 * i + p, p)
            for s in range(2 * (NSLOT // 2), NSLOT + 1):
                tick(s, s % 2)

        def known(s):
            return isinstance(s, int)

        SHARED = NSLOT % 2
        assert SHARED == 1 and EARLY % 2 == 0 and LATE % 2 == 0

        def weights_loaded(s, p):
            return 32 * (1 + p) + 16 * (s - p)

        OUT = [banks[2][:, p * 512:(p + 1) * 512] for p in range(2)]

        @block.sync
        def _(sp):
            sp.dma_start(wr[:], d["L1_ffn_Wr"].rearrange("(k p) e -> p k e", p=P)).then_inc(e_c, 16)
            sp.dma_start(before[:], d["before"]).then_inc(e_c, 16)
            sp.dma_start(e_rank[:], d["e_rank"]).then_inc(e_c, 16)
            sp.dma_start(e_table[:], d["e_table"]).then_inc(e_c, 16)
            sp.dma_start(s_table[:], d["s_table"]).then_inc(e_c, 16)

            def shared1():
                sp.dma_start(w1[SHARED][:].rearrange("p a k f -> p (a k f)"), halves_dram[2 * NE]).then_inc(e_w1[SHARED], 16)
                sp.dma_start(b1[SHARED][:], d["moe_b1s"]).then_inc(e_w1[SHARED], 16)

            def shared2():
                sp.dma_start(w2[SHARED][:].rearrange("p a j c -> p (a j c)"), halves_dram[2 * NE + 1]).then_inc(e_w2[SHARED], 16)
                sp.dma_start(b2[SHARED][:], d["L1_ffn_bproj_s"].rearrange("(a n) -> a n", a=1).to_broadcast([P, D])).then_inc(e_w2[SHARED], 16)

            shared1()
            shared2()
            sp.wait_ge(e_set, 1)
            n = NSLOT * SLOT // P
            sp.dma_start(slots_x.rearrange("(p n) c -> p n c", p=P), zeros[:].rearrange("p (n c) -> p n c", n=1).to_broadcast([P, n, D]))\
              .then_inc(e_zero, 16)

            def expert(s):
                return sp.value_load(slot_e[0:1, bass.ts(s, 1)], min_val=0, max_val=NE - 1)

            def first_weights(s, p):
                e = expert(s)
                wait(sp, e_g, 4 * (EARLY + s - 1) if not (known(s) and s == 0) else 0)
                sp.dma_start(w1[p][:].rearrange("p a k f -> p (a k f)"), halves_dram[bass.ds(2 * e, 1)].rearrange("o p n -> p (o n)")).then_inc(e_w1[p], 16)
                sp.dma_start(b1[p][:], d["moe_b1"][bass.ds(e, 1)].rearrange("o p j -> p (o j)")).then_inc(e_w1[p], 16)

            def second_weights(s, p):
                e = expert(s)
                wait(sp, e_y, EARLY + s - 1 if not (known(s) and s == 0) else 0)
                sp.dma_start(w2[p][:].rearrange("p a j c -> p (a j c)"), halves_dram[bass.ds(2 * e + 1, 1)].rearrange("o p n -> p (o n)")).then_inc(e_w2[p], 16)
                sp.dma_start(b2[p][:], d["L1_ffn_bproj"][bass.ds(e, 1)].to_broadcast([P, D])).then_inc(e_w2[p], 16)

            def slot_rows(s, p):
                wait(sp, e_rt, s - 1)
                sp.dma_start(rows[p][:], slots_x[bass.ts(s, SLOT), :].rearrange("(t p) c -> p t c", p=P)).then_inc(e_r[p], 16)

            def store(s, p):
                sp.wait_ge(e_y, EARLY + s + 1)
                sp.dma_start(slots_y[bass.ts(s, SLOT), :].rearrange("(t p) c -> p t c", p=P), y[p][:]).then_inc(e_st[p], 16)

            sp.wait_ge(e_slot, 1)
            first_weights(0, 0)
            second_weights(0, 0)
            sp.wait_ge(e_sc, 16 * PICKS * NT)
            slot_rows(0, 0)
            slot_rows(1, 1)
            sp.wait_ge(e_g, 4 * EARLY)
            first_weights(1, 1)
            sp.wait_ge(e_b, EARLY)
            second_weights(1, 1)

            def tick(s, p):
                if not (known(s) and s + 2 >= NSLOT):
                    slot_rows(s + 2, p)
                    first_weights(s + 2, p)
                if known(s) and s + 2 == NSLOT:
                    sp.wait_ge(e_g, 4 * (EARLY + NSLOT - 1))
                    shared1()
                if not (known(s) and s < 1):
                    store(s - 1, 1 - p)
                    if not (known(s) and s + 1 >= NSLOT):
                        second_weights(s + 1, 1 - p)
                    if known(s) and s + 1 == NSLOT:
                        sp.wait_ge(e_y, EARLY + NSLOT - 1)
                        shared2()

            for s in range(2):
                tick(s, s)
            with sp.Fori(1, NSLOT // 2 - 1) as i:
                for p in range(2):
                    tick(2 * i + p, p)
            for s in range(2 * (NSLOT // 2 - 1), NSLOT + 1):
                tick(s, s % 2)

        @block.gpsimd
        def _(pool):
            pool.memset(zeros[:], 0.0).then_inc(e_set, 1)
            pool.wait_ge(e_set, 1)
            pool.memset(ones[:], 1.0).then_inc(e_set, 1)
            pool.wait_ge(e_pos, PICKS)
            pool.wait_ge(e_zero, 16)
            for T in range(NT):
                for q in range(PICKS):
                    pool.indirect_dma_start(out=slots_x, out_offset=bass.IndirectOffsetOnAxis(ap=pos[q][:, T:T + 1], axis=0),
                                            in_=xn[:, T, :], in_offset=None).then_inc(e_sc, 16)
            pool.wait_ge(e_sc, 16 * PICKS * NT)
            for p in range(2):
                pool.wait_ge(e_st[p], 16 * ((NSLOT + 1 - p) // 2))
            for T in range(NT):
                for q in range(PICKS):
                    n = PICKS * T + q
                    if n >= RING:
                        pool.wait_ge(e_ad, n - RING + 1)
                    pool.indirect_dma_start(out=ring[n % RING], out_offset=None, in_=slots_y,
                                            in_offset=bass.IndirectOffsetOnAxis(ap=pos[q][:, T:T + 1], axis=0))\
                        .then_inc(e_ga[n % RING], 16)

        def copy_logits(act, c):
            act.wait_ge(e_l, c + 1)
            if c >= 2:
                act.wait_ge(e_lt, c - 1)
            act.activation(lT[c % 2][:], banks[2][0:NE, (c % 2) * 512:(c % 2) * 512 + 512], ACT.Copy).then_inc(e_lc, 1)

        @block.scalar
        def _(act):
            ln_scalar(act, ln, NT, 3)
            act.preload_act_table(ACT.Copy)

            for c in range(NT // TPC):
                act.wait_ge(e_t, c + 1)
                if c >= 2:
                    act.wait_ge(e_l, c - 1)
                src = banks[c % 2][:].rearrange("p (k t) -> p k t", k=KC)
                act.activation(xT32[c % 2][:], src, ACT.Copy).then_inc(e_tc, 1)
                act.activation(xnT[:, 0, :, c * TPC * P:(c + 1) * TPC * P], src, ACT.Copy).then_inc(e_xh, 1)
                if c >= 1:
                    copy_logits(act, c - 1)
            copy_logits(act, NT // TPC - 1)
            act.wait_ge(e_d, 1)
            act.activation(gate[1][:], peak[1][:], ACT.Exp).then_inc(e_e, 1)
            act.preload_act_table(ACT.Gelu_apprx_tanh)

            def copy_rows(s, p):
                act.wait_ge(e_rt, s + 1)
                if not (known(s) and s < 2):
                    act.wait_ge(e_f, 4 * (EARLY + s - 1))
                act.activation(rT[p][:, 0, :, :].rearrange("p k t -> p (k t)"), banks[3][:, 512:1024], ACT.Copy).then_inc(e_rh, 1)

            def gelu(n, p, buffer):
                for jp in range(J // 2):
                    act.wait_ge(e_f, 4 * n + jp + 1)
                    if jp == 0:
                        wait(act, e_hl, 4 * (n - 1))
                    for q in range(2):
                        j = 2 * jp + q
                        src = banks[jp // 2][:, (jp % 2) * 512 + q * SLOT:(jp % 2) * 512 + (q + 1) * SLOT]
                        ins = act.activation(hf[p][:, j, :], src, ACT.Gelu_apprx_tanh, bias=b1[buffer][:, j:j + 1], scale=1.0 / WSCALE)
                    ins.then_inc(e_g, 1)

            def shared_gelus(base, count):
                for c in range(2):
                    gelu(base + c, (base + c) % 2, SHARED)
                with act.Fori(1, count // 2) as i:
                    for p in range(2):
                        gelu(base + 2 * i + p, (base + p) % 2, SHARED)

            def tick(s, p):
                if not (known(s) and s + 1 >= NSLOT):
                    copy_rows(s + 1, 1 - p)
                if not (known(s) and s >= NSLOT):
                    gelu(EARLY + s, p, p)

            act.wait_ge(e_w1[SHARED], 32)
            shared_gelus(0, EARLY)
            copy_rows(0, 0)
            walk(act, tick)
            act.wait_ge(e_w1[SHARED], weights_loaded(NSLOT, SHARED))
            shared_gelus(EARLY + NSLOT, LATE)

        def chunk_logits(pe, c):
            pe.wait_ge(e_tc, c + 1)
            if c >= 2:
                pe.wait_ge(e_lc, c - 1)
            for k in range(KC):
                ins = pe.matmul(banks[2][0:NE, (c % 2) * 512:(c % 2) * 512 + 512], wr[:, k, :], xT32[c % 2][:, k, :],
                                start=(k == 0), stop=(k == KC - 1))
            ins.then_inc(e_l, 1)

        def turn(pe, c):
            pe.wait_ge(e_lc, c + 1)
            for t in range(TPC):
                T = TPC * c + t
                ins = pe.transpose(banks[3][:, T * NE:(T + 1) * NE], lT[c % 2][:, t * P:(t + 1) * P], ident[0:NE, 0:NE])
            ins.then_inc(e_lt, 1)

        PARTS = ((0, 0), (0, 1), (1, 0))

        @block.tensor
        def _(pe):
            pe.wait_ge(e_c, 16 * 5)
            for c in range(NT // TPC):
                pe.wait_ge(e_xn, TPC * (c + 1))
                if c >= 2:
                    pe.wait_ge(e_tc, c - 1)
                    pe.wait_ge(e_xh, c - 1)
                    pe.wait_ge(e_xl, c - 1)
                for k in range(KC):
                    for t in range(TPC):
                        ins = pe.transpose(banks[c % 2][:, k * 512 + t * P:k * 512 + (t + 1) * P], xn[:, TPC * c + t, k * P:(k + 1) * P], ident[:])
                ins.then_inc(e_t, 1)
                if c:
                    chunk_logits(pe, c - 1)
                if c > 1:
                    turn(pe, c - 2)
            chunk_logits(pe, NT // TPC - 1)
            turn(pe, NT // TPC - 2)
            turn(pe, NT // TPC - 1)
            pe.wait_ge(e_m, 1)
            pe.wait_ge(e_set, 2)
            pe.matmul(banks[2][:, 0:NT * NE], before[:], tmp[:].rearrange("p t e -> p (t e)"), start=True, stop=True)
            pe.matmul(banks[2][:, 512:512 + NT * NE], ones[:], tmp[:].rearrange("p t e -> p (t e)"), start=True, stop=True).then_inc(e_p, 1)
            pe.wait_ge(e_pos, PICKS)
            pe.wait_ge(e_xh, NT // TPC)
            pe.wait_ge(e_xl, NT // TPC)

            def rows_T(s, p):
                pe.wait_ge(e_r[p], 8 * (s - p) + 16)
                wait(pe, e_rl, s)
                for k in range(KC):
                    for t in range(ST):
                        ins = pe.transpose(banks[3][:, 512 + (k * ST + t) * P:512 + (k * ST + t + 1) * P], rows[p][:, t, k * P:(k + 1) * P], ident[:])
                ins.then_inc(e_rt, 1)

            def first(n, buffer, moving):
                for jp in range(J // 2):
                    wait(pe, e_g, 4 * (n - 1) + jp + 1)
                    for q in range(2):
                        j = 2 * jp + q
                        at = (jp % 2) * 512 + q * SLOT
                        for k in range(KC):
                            for w, x in PARTS:
                                ins = pe.matmul(banks[jp // 2][:, at:at + SLOT], w1[buffer][:, w, k, j * P:(j + 1) * P], moving(x, k),
                                                start=(k == 0 and (w, x) == PARTS[0]), stop=(k == KC - 1 and (w, x) == PARTS[-1]))
                    ins.then_inc(e_f, 1)

            def second(n, p, buffer):
                pe.wait_ge(e_hl, 4 * n + 4)
                wait(pe, e_y, n - 1)
                for t in range(ST):
                    for j in range(J):
                        for w, x in PARTS:
                            ins = pe.matmul(OUT[p][:, t * D:(t + 1) * D], hT[p][:, x, j, t * P:(t + 1) * P], w2[buffer][:, w, j, :],
                                            start=(j == 0 and (w, x) == PARTS[0]), stop=(j == J - 1 and (w, x) == PARTS[-1]))
                ins.then_inc(e_o, 1)

            def shared_chunks(base, chunk0, count):
                def one(c):
                    first(base + c, SHARED, lambda x, k: xnT[:, x, k, bass.ts(c + chunk0, SLOT)])
                q = base % 2
                one(0)
                one(1)
                second(base, q, SHARED)
                with pe.Fori(1, count // 2) as i:
                    one(2 * i)
                    second(base + 2 * i - 1, 1 - q, SHARED)
                    one(2 * i + 1)
                    second(base + 2 * i, q, SHARED)
                second(base + count - 1, 1 - q, SHARED)

            pe.wait_ge(e_w1[SHARED], 32)
            pe.wait_ge(e_w2[SHARED], 32)
            shared_chunks(0, 0, EARLY)

            def tick(s, p):
                if not (known(s) and s + 1 >= NSLOT):
                    rows_T(s + 1, 1 - p)
                if not (known(s) and s >= NSLOT):
                    pe.wait_ge(e_w1[p], weights_loaded(s, p))
                    pe.wait_ge(e_rl, s + 1)
                    first(EARLY + s, p, lambda x, k: rT[p][:, x, k, :])
                if not (known(s) and s < 1):
                    pe.wait_ge(e_w2[1 - p], weights_loaded(s - 1, 1 - p))
                    second(EARLY + s - 1, 1 - p, 1 - p)

            rows_T(0, 0)
            walk(pe, tick)
            pe.wait_ge(e_w1[SHARED], weights_loaded(NSLOT, SHARED))
            pe.wait_ge(e_w2[SHARED], weights_loaded(NSLOT, SHARED))
            shared_chunks(EARLY + NSLOT, EARLY, LATE)

        @block.vector
        def _(v):
            ln_vector(v, ln, X, NT, D, 3)
            with v.Fori(0, NT) as T:
                v.tensor_scalar(xn[:, T, :], X[:, T, :], ln["rstd"][:, bass.ts(T, 1)], ln["nmr"][:, bass.ts(T, 1)],
                                ALU.mult, ALU.add).then_inc(e_xn, 1)
            for c in range(NT // TPC):
                at = slice(c * TPC * P, (c + 1) * TPC * P)
                v.wait_ge(e_xh, c + 1)
                v.tensor_tensor(xnT[:, 1, :, at], banks[c % 2][:].rearrange("p (k t) -> p k t", k=KC), xnT[:, 0, :, at], ALU.subtract)\
                 .then_inc(e_xl, 1)
            done = 0

            def link(ins):
                nonlocal done
                ins.then_inc(e_v, 1)
                done += 1
                v.wait_ge(e_v, done)

            def over(a, shape, axis):
                return a.rearrange("p t -> p t ()" if axis == 2 else "p e -> p () e").to_broadcast(shape)

            full = [P, NT, NE]
            v.wait_ge(e_c, 16 * 5)
            v.wait_ge(e_lt, NT // TPC)
            link(v.tensor_copy(logit[:].rearrange("p t e -> p (t e)"), banks[3][:, 0:NT * NE]))
            for q in range(PICKS):
                link(v.tensor_reduce(peak[q][:], logit[:], AX.X, ALU.max))
                link(v.tensor_tensor(tmp[:], logit[:], over(peak[q][:], full, 2), ALU.is_equal))
                link(v.tensor_tensor(tmp[:], tmp[:], over(e_rank[:], full, 1), ALU.mult))
                link(v.tensor_reduce(pick[:], tmp[:], AX.X, ALU.max))
                link(v.tensor_tensor(hot[q][:], over(e_rank[:], full, 1), over(pick[:], full, 2), ALU.is_equal))
                if q == 0:
                    link(v.scalar_tensor_tensor(logit[:], hot[0][:], -3e38, logit[:], ALU.mult, ALU.add))
            link(v.tensor_tensor(tmp[:], hot[0][:], hot[1][:], ALU.add))
            v.tensor_tensor(peak[1][:], peak[1][:], peak[0][:], ALU.subtract).then_inc(e_d, 1)
            v.wait_ge(e_d, 1)
            v.sem_inc(e_m, 1)
            v.wait_ge(e_e, 1)
            link(v.tensor_scalar(gate[0][:], gate[1][:], 1.0, None, ALU.add))
            link(v.reciprocal(gate[0][:], gate[0][:]))
            link(v.tensor_tensor(gate[1][:], gate[1][:], gate[0][:], ALU.mult))
            v.wait_ge(e_p, 1)
            link(v.tensor_copy(total[:].rearrange("p t e -> p (t e)"), banks[2][:, 512:512 + NT * NE]))
            src, step, n = total, 1, 0
            while step < NT:
                dst = tot[n % 2]
                v.tensor_copy(dst[:, 0:step, :], src[:, 0:step, :])
                link(v.tensor_tensor(dst[:, step:NT, :], src[:, step:NT, :], src[:, 0:NT - step, :], ALU.add))
                src, step, n = dst, 2 * step, n + 1
            link(v.tensor_tensor(cmp_e[:], src[:, NT - 1, :].rearrange("p e -> p e ()").to_broadcast([P, NE, MOST]), e_table[:], ALU.is_gt))
            link(v.tensor_reduce(n_slots[:], cmp_e[:], AX.X, ALU.add))
            link(v.memset(start[:, 0:1], 0.0))
            for e in range(NE):
                link(v.tensor_tensor(start[:, e + 1:e + 2], start[:, e:e + 1], n_slots[:, e:e + 1], ALU.add))
            link(v.tensor_tensor(cmp_s[:], s_table[:], start[:, 0:NE].rearrange("p e -> p () e").to_broadcast([P, NSLOT, NE]), ALU.is_ge))
            link(v.tensor_reduce(slot_ef[:], cmp_s[:], AX.X, ALU.add))
            v.tensor_scalar(slot_e[:], slot_ef[:], 1.0, None, ALU.subtract).then_inc(e_slot, 1)
            link(v.tensor_tensor(base[:], src[:], total[:], ALU.subtract))
            link(v.tensor_tensor(base[:].rearrange("p t e -> p (t e)"), base[:].rearrange("p t e -> p (t e)"), banks[2][:, 0:NT * NE], ALU.add))
            link(v.scalar_tensor_tensor(base[:], over(start[:, 0:NE], full, 1), float(SLOT), base[:], ALU.mult, ALU.add))
            for q in range(PICKS):
                link(v.tensor_tensor(hot[q][:], hot[q][:], base[:], ALU.mult))
                link(v.tensor_reduce(posf[q][:], hot[q][:], AX.X, ALU.add))
                v.tensor_copy(pos[q][:], posf[q][:]).then_inc(e_pos, 1)

            def low_rows(s, p):
                v.wait_ge(e_rh, s + 1)
                v.tensor_tensor(rT[p][:, 1, :, :].rearrange("p k t -> p (k t)"), banks[3][:, 512:1024],
                                rT[p][:, 0, :, :].rearrange("p k t -> p (k t)"), ALU.subtract).then_inc(e_rl, 1)

            def cut(n, p):
                for jp in range(J // 2):
                    at = slice(2 * jp, 2 * jp + 2)
                    v.wait_ge(e_g, 4 * n + jp + 1)
                    if jp == 0:
                        wait(v, e_o, n - 1)
                    v.tensor_copy(hT[p][:, 0, at, :], hf[p][:, at, :]).then_inc(e_hh, 1)
                    v.wait_ge(e_hh, 4 * n + jp + 1)
                    v.tensor_tensor(hT[p][:, 1, at, :], hf[p][:, at, :], hT[p][:, 0, at, :], ALU.subtract).then_inc(e_hl, 1)

            def output(s, p):
                v.wait_ge(e_o, EARLY + s + 1)
                if not (known(s) and s < 2):
                    v.wait_ge(e_st[p], 8 * (s - p))
                v.wait_ge(e_w2[p], weights_loaded(s, p))
                v.scalar_tensor_tensor(y[p][:], OUT[p].rearrange("p (t c) -> p t c", t=ST), 1.0 / WSCALE,
                                       b2[p][:].rearrange("p c -> p () c").to_broadcast([P, ST, D]), ALU.mult, ALU.add).then_inc(e_y, 1)

            def shared_output(n, p, chunk):
                at = bass.ts(chunk, ST)
                v.wait_ge(e_o, n + 1)
                v.scalar_tensor_tensor(X[:, at, :], OUT[p].rearrange("p (t c) -> p t c", t=ST), 1.0 / WSCALE, X[:, at, :], ALU.mult, ALU.add)\
                 .then_inc(e_y, 1)
                v.wait_ge(e_y, n + 1)
                v.tensor_tensor(X[:, at, :], X[:, at, :], b2[SHARED][:].rearrange("p c -> p () c").to_broadcast([P, ST, D]), ALU.add).then_inc(e_b, 1)

            v.wait_ge(e_w2[SHARED], 32)
            cut(0, 0)
            cut(1, 1)
            shared_output(0, 0, 0)
            with v.Fori(1, EARLY // 2) as i:
                cut(2 * i, 0)
                shared_output(2 * i - 1, 1, 2 * i - 1)
                cut(2 * i + 1, 1)
                shared_output(2 * i, 0, 2 * i)
            shared_output(EARLY - 1, 1, EARLY - 1)
            v.wait_ge(e_b, EARLY)

            def tick(s, p):
                if not (known(s) and s + 1 >= NSLOT):
                    low_rows(s + 1, 1 - p)
                if not (known(s) and s >= NSLOT):
                    cut(EARLY + s, p)
                if not (known(s) and s < 1):
                    output(s - 1, 1 - p)

            low_rows(0, 0)
            walk(v, tick)

            v.wait_ge(e_w2[SHARED], weights_loaded(NSLOT, SHARED))
            late = EARLY + NSLOT
            cut(late, late % 2)
            for c in range(LATE):
                if c + 1 < LATE:
                    cut(late + c + 1, (late + c + 1) % 2)
                shared_output(late + c, (late + c) % 2, EARLY + c)
                v.wait_ge(e_b, EARLY + c + 1)
                for T in range(NT * c // LATE, NT * (c + 1) // LATE):
                    for q in range(PICKS):
                        n = PICKS * T + q
                        v.wait_ge(e_ga[n % RING], 16 * (n // RING + 1))
                        v.scalar_tensor_tensor(X[:, T, :], ring[n % RING], gate[q][:, T:T + 1], X[:, T, :], ALU.mult, ALU.add).then_inc(e_ad, 1)
                        v.wait_ge(e_ad, n + 1)


def program(nc, d, out):
    g = Shape(d)
    with ExitStack() as ctx:
        g.passed_vector = ctx.enter_context(nc.semaphore("passed_vector"))
        g.passed_pool = ctx.enter_context(nc.semaphore("passed_pool"))
        g.ln = ln_memory(ctx, nc, g.NT)
        X = ctx.enter_context(nc.sbuf_tensor("X", [P, g.NT, g.D], F32))
        ident = ctx.enter_context(nc.sbuf_tensor("ident", [P, P], F32))
        banks = [ctx.enter_context(nc.psum_tensor(f"banks{i}", [P, 1024], F32)) for i in range(4)]
        NE, _, F = d["L1_ffn_Wfc"].shape
        halves_dram = nc.dram_tensor("moe_halves", [2 * (NE + 1), P, 2 * g.D * F // P], F16).ap()
        if STAGE_FROM == 0:
            attention(nc, d, g, X, ident, banks, halves_dram)
            quant_mlp(nc, d, g, X, ident, banks)
            autocorrelation(nc, d, g, X, ident, banks)
            moe(nc, d, g, X, ident, banks, halves_dram)
        store(nc, out, g, X)


def store(nc, out, g, X):
    with ExitStack() as ctx:
        s_out = ctx.enter_context(nc.semaphore("out_stored"))
        block = ctx.enter_context(nc.Block())

        @block.sync
        def _(sp):
            sp.dma_start(out.rearrange("b (t p) c -> p (b t) c", p=P), X[:]).then_inc(s_out, 16)
            sp.wait_ge(s_out, 16)


def fourier(NB, S, D):
    import numpy as np
    h = S // 2
    t = np.arange(S)
    angle = 2 * np.pi * np.outer(t, np.arange(h)) / S
    sine = np.sin(angle)
    sine[:, 0] = np.cos(np.pi * t)
    lag = (S - 1 - t) % S
    back = 2 * np.pi * np.outer(np.arange(h), lag) / S
    like = 2 * np.cos(back)
    even, odd, cross = like.copy(), like.copy(), 2 * np.sin(back)
    even[0], odd[0], cross[0] = 1, np.cos(np.pi * lag), 0
    scale = 1.0 / (S * D)
    f = np.float32
    dc = np.zeros((P, 1), f)
    dc[0] = S
    cosine_sine = np.concatenate([np.cos(angle), sine], axis=1).astype(f)
    return {
        "dft_flipped": np.ascontiguousarray(cosine_sine.reshape(-1, P, S)[:, ::-1].reshape(S, S)),
        "flip": np.ascontiguousarray(np.eye(P, dtype=f)[::-1]),
        "dft": cosine_sine,
        "idft": (np.concatenate([even, odd, cross]) * scale).astype(f),
        "lag_rank": np.tile((t + 1).astype(f), (NB, 1)),
        "dc": dc,
    }


def routing_tables(tokens, NE):
    import numpy as np
    SLOT = 256
    nslot = (2 * tokens + NE * (SLOT - 1)) // SLOT
    f = np.float32
    return {
        "before": np.triu(np.ones((P, P), f), 1),
        "e_rank": np.tile(np.arange(NE, 0, -1).astype(f), (P, 1)),
        "e_table": np.ascontiguousarray(np.broadcast_to((np.arange(tokens // SLOT) * SLOT).astype(f), (P, NE, tokens // SLOT))),
        "s_table": np.ascontiguousarray(np.broadcast_to(np.arange(nslot).astype(f)[:, None], (P, nslot, NE))),
    }


def kernel(**inputs):
    import numpy as np
    import concourse.bacc as bacc
    from concourse.bass_utils import run_bass_kernel_spmd as run

    nc = bacc.Bacc("TRN2", target_bir_lowering=False, num_devices=1)
    arrays = {k: np.ascontiguousarray(a) for k, a in inputs.items()}
    arrays["wo0T"] = np.ascontiguousarray(np.asarray(inputs["L0_xattn_W_out"]).T)
    arrays["ident"] = np.eye(P, dtype=np.float32)
    arrays["ffn_b1"] = np.ascontiguousarray(np.asarray(inputs["L0_ffn_b1"]).reshape(-1, P).T)
    w = {k: np.asarray(inputs["L1_xattn_" + k]) for k in ("Wq", "bq", "Wk", "bk", "Wv", "bv")}
    arrays["wkT"] = np.ascontiguousarray(w["Wk"].T)
    arrays["wvT"] = np.ascontiguousarray(w["Wv"].T)
    arrays["wqTb"] = np.ascontiguousarray(np.concatenate([w["Wq"].T, w["bq"][:, None]], axis=1))
    arrays["bk"] = np.ascontiguousarray(w["bk"].reshape(-1, P).T)
    arrays["bv"] = np.ascontiguousarray(w["bv"].reshape(-1, P).T)
    arrays.update(fourier(*arrays["x"].shape))
    NE, D, F = arrays["L1_ffn_Wfc"].shape
    arrays["moe_b1"] = np.ascontiguousarray(arrays["L1_ffn_bfc"].reshape(NE, -1, P).transpose(0, 2, 1))
    arrays["moe_b1s"] = np.ascontiguousarray(arrays["L1_ffn_bfc_s"].reshape(-1, P).T)
    arrays.update(routing_tables(arrays["x"].shape[0] * arrays["x"].shape[1], NE))
    d = {k: nc.dram_tensor(f"in_{k}", a.shape, mybir.dt.from_np(a.dtype), kind="ExternalInput").ap() for k, a in arrays.items()}
    shape = arrays["x"].shape
    out = nc.dram_tensor("out_x", shape, F32, kind="ExternalOutput").ap()
    program(nc, d, out)
    r = run(nc, [{f"in_{k}": a for k, a in arrays.items()}], core_ids=[0])
    return r.results[0]["out_x"]
```
